# Optimizing a Trainium2 kernel written in Bass

```python
import numpy as np
import jax
import jax.numpy as jnp

def _softmax(x, axis=-1):
    return jax.nn.softmax(x, axis=axis)

def _gelu(x):
    return jax.nn.gelu(x, approximate=True)

def _silu(x):
    return jax.nn.silu(x)

def _sigmoid(x):
    return jax.nn.sigmoid(x)

def _layernorm(x, axis=-1, eps=1e-05):
    m = jnp.mean(x, axis=axis, keepdims=True)
    v = jnp.var(x, axis=axis, keepdims=True)
    return (x - m) / jnp.sqrt(v + eps)

def _scatter_add(tgt, idx, src, axis=0):
    return tgt.at[idx].add(src)

def _segment_sum(src, seg, n):
    return jax.ops.segment_sum(src, seg, n)
kernel_name = 'mk_adaln_ffn_d1_seqx_r4_834c9c'

def setup_inputs(seed: int=0):
    np.random.seed(seed)
    _w = jnp.asarray

    def _rec_inputs():
        import jax
        import jax.numpy as jnp
        _rk = jax.random.key(seed)
        x = 7.971e-05 + 1 * jax.random.normal(jax.random.fold_in(_rk, 1), (16, 256, 256), jnp.float32)
        _lenS = 256 - jax.random.randint(jax.random.fold_in(_rk, 7), (16,), 0, max(1, 256 // 4) + 1, jnp.int32)
        _lenS2 = 256 - jax.random.randint(jax.random.fold_in(_rk, 8), (16,), 0, max(1, 256 // 4) + 1, jnp.int32)
        itok_B_0_6 = jax.random.randint(jax.random.fold_in(_rk, 11), (16,), 0, 7, jnp.int32)
        return (x, itok_B_0_6)
    x, itok_B_0_6 = _rec_inputs()

    def _L0_cond_setup():
        import jax, jax.numpy as jnp
        import numpy as np
        N_PROFILES = 8
        HIDDEN = 256
        BOTTLENECK = 128
        EPS = 1e-05
        key = jax.random.key(seed)
        ks = jax.random.split(key, 8)
        B, S, H, K, P = (16, 512, HIDDEN, BOTTLENECK, N_PROFILES)
        down_w = jax.random.normal(ks[0], (P, H, K), dtype=jnp.float32) * (1.0 / np.sqrt(H))
        down_b = jax.random.normal(ks[1], (P, K), dtype=jnp.float32) * 0.01
        up_w = jax.random.normal(ks[2], (P, K, H), dtype=jnp.float32) * (1.0 / np.sqrt(K))
        up_b = jax.random.normal(ks[3], (P, H), dtype=jnp.float32) * 0.01
        ln_g = jnp.ones((P, H), dtype=jnp.float32)
        ln_b = jnp.zeros((P, H), dtype=jnp.float32)
        hidden = jax.random.normal(ks[4], (B, S, H), dtype=jnp.float32)
        profile_ids = jax.random.randint(ks[5], (B,), 0, P)
        return {'hidden': hidden, 'profile_ids': profile_ids, 'down_w': down_w, 'down_b': down_b, 'up_w': up_w, 'up_b': up_b, 'ln_g': ln_g, 'ln_b': ln_b}
    _L0_cond_all = _L0_cond_setup()
    _L0_cond_in = {k: v for k, v in _L0_cond_all.items() if k in ('down_w', 'down_b', 'up_w', 'up_b', 'ln_g', 'ln_b')}
    del _L0_cond_all

    def _L0_ffn_setup():
        import jax, jax.numpy as jnp
        import numpy as np
        BS, L, D = (4, 512, 256)
        H, E, K = (8, 16, 2)
        HD = D // H
        I = 1024 // H
        key = jax.random.key(seed)
        ks = jax.random.split(key, 10)
        s = lambda k, shp, fan: jax.random.normal(k, shp, jnp.float32) / np.sqrt(fan)
        return {'x': jax.random.normal(ks[0], (BS, L, D), jnp.float32), 'Wm': s(ks[1], (D, D), D), 'bm': jnp.zeros((D,), jnp.float32), 'expert_emb': jax.random.normal(ks[2], (HD, E), jnp.float32), 'W1': s(ks[3], (E, HD, I), HD), 'b1': jnp.zeros((E, I), jnp.float32), 'W2': s(ks[4], (E, I, HD), I), 'b2': jnp.zeros((E, HD), jnp.float32), 'Wo': s(ks[5], (D, D), D), 'bo': jnp.zeros((D,), jnp.float32)}
    _L0_ffn_all = _L0_ffn_setup()
    _L0_ffn_in = {k: v for k, v in _L0_ffn_all.items() if k in ('Wm', 'bm', 'expert_emb', 'W1', 'b1', 'W2', 'b2', 'Wo', 'bo')}
    del _L0_ffn_all
    return {'x': x, 'itok_B_0_6': itok_B_0_6, 'L0_cond_down_w': _L0_cond_in['down_w'], 'L0_cond_down_b': _L0_cond_in['down_b'], 'L0_cond_up_w': _L0_cond_in['up_w'], 'L0_cond_up_b': _L0_cond_in['up_b'], 'L0_cond_ln_g': _L0_cond_in['ln_g'], 'L0_cond_ln_b': _L0_cond_in['ln_b'], 'L0_ffn_Wm': _L0_ffn_in['Wm'], 'L0_ffn_bm': _L0_ffn_in['bm'], 'L0_ffn_expert_emb': _L0_ffn_in['expert_emb'], 'L0_ffn_W1': _L0_ffn_in['W1'], 'L0_ffn_b1': _L0_ffn_in['b1'], 'L0_ffn_W2': _L0_ffn_in['W2'], 'L0_ffn_b2': _L0_ffn_in['b2'], 'L0_ffn_Wo': _L0_ffn_in['Wo'], 'L0_ffn_bo': _L0_ffn_in['bo']}

def reference(x, itok_B_0_6, L0_cond_down_w, L0_cond_down_b, L0_cond_up_w, L0_cond_up_b, L0_cond_ln_g, L0_cond_ln_b, L0_ffn_Wm, L0_ffn_bm, L0_ffn_expert_emb, L0_ffn_W1, L0_ffn_b1, L0_ffn_W2, L0_ffn_b2, L0_ffn_Wo, L0_ffn_bo):
    import jax
    import jax.numpy as jnp

    def _L0_cond_ref(hidden, profile_ids, down_w, down_b, up_w, up_b, ln_g, ln_b):
        import jax, jax.numpy as jnp
        import numpy as np
        N_PROFILES = 8
        HIDDEN = 256
        BOTTLENECK = 128
        EPS = 1e-05
        Wd = down_w[profile_ids]
        bd = down_b[profile_ids][:, None]
        Wu = up_w[profile_ids]
        bu = up_b[profile_ids][:, None]
        g = ln_g[profile_ids][:, None]
        b = ln_b[profile_ids][:, None]
        z = jax.nn.relu(jnp.einsum('bsh,bhk->bsk', hidden, Wd) + bd)
        y = hidden + jnp.einsum('bsk,bkh->bsh', z, Wu) + bu
        mu = jnp.mean(y, axis=-1, keepdims=True)
        var = jnp.mean(jnp.square(y - mu), axis=-1, keepdims=True)
        return (y - mu) * jax.lax.rsqrt(var + EPS) * g + b

    def _L0_ffn_ref(x, Wm, bm, expert_emb, W1, b1, W2, b2, Wo, bo):
        import jax, jax.numpy as jnp
        import numpy as np
        BS, L, D = (4, 512, 256)
        H, E, K = (8, 16, 2)
        HD = D // H
        I = 1024 // H
        bs, L_, d = x.shape
        h = x @ Wm + bm
        t = h.reshape(bs * L_ * H, HD)
        logits = t @ expert_emb
        w = jax.nn.softmax(logits, axis=-1)
        topw, topi = jax.lax.top_k(w, K)
        hmid = jax.nn.gelu(jnp.einsum('td,edi->tei', t, W1) + b1, approximate=False)
        eo = jnp.einsum('tei,eio->teo', hmid, W2) + b2
        sel = jnp.take_along_axis(eo, topi[:, :, None], axis=1)
        comb = (sel * topw[:, :, None]).sum(axis=1)
        out = comb.reshape(bs, L_, d)
        return out @ Wo + bo
    x = x + _L0_ffn_ref(_L0_cond_ref(x, itok_B_0_6, L0_cond_down_w, L0_cond_down_b, L0_cond_up_w, L0_cond_up_b, L0_cond_ln_g, L0_cond_ln_b), L0_ffn_Wm, L0_ffn_bm, L0_ffn_expert_emb, L0_ffn_W1, L0_ffn_b1, L0_ffn_W2, L0_ffn_b2, L0_ffn_Wo, L0_ffn_bo)
    return x

_drawn_inputs = setup_inputs


def setup_inputs(seed=0):
    import zlib

    import numpy as np

    out = dict(_drawn_inputs(seed))
    spreads = {'L0_cond_ln_g': (1.0, 0.2),
     'L0_cond_ln_b': (0.0, 0.1),
     'L0_ffn_bm': (0.0, 0.1),
     'L0_ffn_b1': (0.0, 0.1),
     'L0_ffn_b2': (0.0, 0.1),
     'L0_ffn_bo': (0.0, 0.1)}
    factors = {'L0_cond_down_b': 4.794, 'L0_cond_up_b': 3.862}
    for name, (base, spread) in spreads.items():
        noise = np.random.default_rng([zlib.crc32(name.encode()), seed]).standard_normal(out[name].shape)
        drawn = base * np.exp(spread * noise) if base else spread * noise
        out[name] = jnp.asarray(drawn.astype(out[name].dtype))
    for name, factor in factors.items():
        out[name] = (out[name] * factor).astype(out[name].dtype)
    return out
```

```python
from contextlib import ExitStack

import concourse.bass as bass
from concourse import mybir

F32 = mybir.dt.float32
F32R = mybir.dt.float32r
I32 = mybir.dt.int32
ALU = mybir.AluOpType
ACT = mybir.ActivationFunctionType
AX_X = mybir.AxisListType.X

P = 128
SAMPLES, TOK, D = 16, 256, 256
T2 = TOK // P
CC = D // P
PROFILES, NECK = 8, 128
HEADS, HD = 8, 32
EXPERTS, HID = 16, 128
EPS = 1e-5
CHUNK = 1024
SPC = CHUNK // TOK
CHUNKS = SAMPLES // SPC
UNITS = CHUNKS * HEADS
HALF = 512
GROUPS, GE = 4, 4
HPT = P // HD
HE = HEADS * EXPERTS
RING = 4
LEAD = SPC + 1

DOWN, UP, DB, LG, LB, UB = 0, 256, 512, 513, 515, 517
PW = UB + D


def at_least(eng, sem, value):
    if not isinstance(value, int) or value > 0:
        eng.wait_ge(sem, value)


def carried(eng, ticks):
    eng.sem_inc(ticks, 1)


def build(nc, x, ids, prof, wm, bm, emb, w1, b1, w2, b2, wo, bo, ident, sel, rank, out):
    with ExitStack() as ctx:
        def sb(name, shape, dt=F32):
            return ctx.enter_context(nc.sbuf_tensor(name, shape, dt))

        def sem(name):
            return ctx.enter_context(nc.semaphore(name))

        parts_d = nc.dram_tensor("parts_scratch", (CHUNKS, HEADS, 2, HD, CHUNK), F32, kind="Internal").ap()
        route_d = nc.dram_tensor("route_scratch", (CHUNKS, HE, CHUNK), F32, kind="Internal").ap()
        mixed_d = nc.dram_tensor("mixed_scratch", (CHUNKS, HEADS * HD, CHUNK), F32, kind="Internal").ap()

        psum = ctx.enter_context(nc.psum_tensor("psum", [P, 8, HALF], F32))

        ids_s = sb("ids_s", [1, SAMPLES], I32)
        wm_s = sb("wm_s", [P, CC, D])
        bm_s = sb("bm_s", [P, CC])
        emb_s = sb("emb_s", [P, HPT * EXPERTS])
        w1_raw = sb("w1_raw", [P, EXPERTS, HID])
        w1_s = sb("w1_s", [P, EXPERTS, HID], F32R)
        b1_s = sb("b1_s", [P, EXPERTS])
        w2_s = sb("w2_s", [P, EXPERTS, HD])
        b2_s = sb("b2_s", [P, GROUPS])
        wo_s = sb("wo_s", [P, CC, D])
        bo_s = sb("bo_s", [P, D])
        ident_s = sb("ident_s", [P, P])
        sel_s = sb("sel_s", [P, HD])
        rank_s = sb("rank_s", [P, TOK])
        minus_half = sb("minus_half", [P, T2])
        eps_s = sb("eps_s", [P, T2])

        xin = [sb(f"xin{i}", [P, T2, D]) for i in range(RING)]
        pf = [sb(f"pf{i}", [P, PW]) for i in range(RING)]
        xb = [sb(f"xb{i}", [P, T2, D]) for i in range(2)]
        xT = sb("xT", [P, CC, TOK])
        zT = sb("zT", [P, TOK])
        y = [sb(f"y{i}", [P, T2, D]) for i in range(2)]
        stats = sb("stats", [P, T2, 6])
        mv = [sb(f"mv{i}", [P, T2, 2]) for i in range(2)]
        vareps = sb("vareps", [P, T2])
        rstd = [sb(f"rstd{i}", [P, T2]) for i in range(2)]
        yn = sb("yn", [P, T2, D])
        ynT = sb("ynT", [P, CC, TOK])
        hT = [sb(f"hT{i}", [P, CC, TOK]) for i in range(2)]
        hi = [sb(f"hi{i}", [P, CC, TOK], F32R) for i in range(2)]
        lo = [sb(f"lo{i}", [P, CC, TOK], F32R) for i in range(2)]
        lmax = sb("lmax", [P, T2 * HEADS])
        ldiff = sb("ldiff", [P, TOK])
        prob = sb("prob", [P, SAMPLES, T2 * HE])

        t_p = sb("t_p", [P, T2 * HE])
        t_q = sb("t_q", [P, T2 * HE])
        t_s = sb("t_s", [P, T2 * HE])
        t_one = sb("t_one", [P, T2 * HE])
        t_rest = sb("t_rest", [P, T2 * HE])
        t_two = sb("t_two", [P, T2 * HE])
        t_m = sb("t_m", [P, T2 * HEADS])
        t_z = sb("t_z", [P, T2 * HEADS])
        t_rz = sb("t_rz", [P, T2 * HEADS])
        route = sb("route", [P, T2 * HE])
        routeT = sb("routeT", [P, TOK])

        parts = [sb(f"parts{i}", [P, CHUNK], F32R) for i in range(2)]
        wb = [sb(f"wb{i}", [P, GROUPS, CHUNK]) for i in range(2)]
        hid = [sb(f"hid{i}", [P, GE, CHUNK]) for i in range(2)]
        wout = sb("wout", [P, GROUPS, CHUNK])
        total = [sb(f"total{i}", [P, CHUNK]) for i in range(2)]
        mixed = [sb(f"mixed{i}", [P, TOK]) for i in range(2)]
        mixT = sb("mixT", [P, CC, TOK])
        xres = sb("xres", [P, T2, D])
        fin = sb("fin", [P, T2, D])

        ids_loaded, head_consts, tail_consts = sem("ids_loaded"), sem("head_consts"), sem("tail_consts")
        x_loaded = [sem(f"x_loaded{i}") for i in range(RING)]
        pf_loaded = [sem(f"pf_loaded{i}") for i in range(RING)]
        parts_stored = [sem(f"parts_stored{i}") for i in range(2)]
        route_stored, mixed_stored, out_stored = sem("route_stored"), sem("mixed_stored"), sem("out_stored")
        parts_loaded, wb_loaded = sem("parts_loaded"), sem("wb_loaded")
        mixT_loaded, xres_loaded = sem("mixT_loaded"), sem("xres_loaded")
        half_set = sem("half_set")
        sp_ticks, dve_ticks = sem("sp_ticks"), sem("dve_ticks")
        w1_high, w1_split = sem("w1_high"), sem("w1_split")
        xb_ready = sem("xb_ready")
        xT_done, xT_ready = sem("xT_done"), sem("xT_ready")
        z_done, z_ready = sem("z_done"), sem("z_ready")
        y_done, y_ready = sem("y_done"), sem("y_ready")
        stats_ready, mv_ready = sem("stats_ready"), sem("mv_ready")
        rstd_step = sem("rstd_step")
        yn_ready = sem("yn_ready")
        ynT_done, ynT_ready = sem("ynT_done"), sem("ynT_ready")
        hT_done, hT_ready = sem("hT_done"), sem("hT_ready")
        hi_ready, lo_ready = sem("hi_ready"), sem("lo_ready")
        logits_done, lmax_ready, ldiff_ready = sem("logits_done"), sem("lmax_ready"), sem("ldiff_ready")
        prob_ready = sem("prob_ready")
        choose_step = sem("choose_step")
        routeT_done, routeT_ready = sem("routeT_done"), sem("routeT_ready")
        hidden_done = sem("hidden_done")
        gelu_done = sem("gelu_done")
        expert_done = sem("expert_done")
        weighted = sem("weighted")
        summed = sem("summed")
        mixed_done, mixed_ready = sem("mixed_done"), sem("mixed_ready")
        proj_done, xres_biased, fin_ready = sem("proj_done"), sem("xres_biased"), sem("fin_ready")

        B_LOGIT, B_XT, B_YNT, B_Z, B_HT, B_Y = range(6)
        B_OUT, B_MIX, B_AUX = 4, 6, 7

        def back(b, k, lag):
            return b + (k - lag) // RING, (k - lag) % RING

        def steps(eng, step):
            for k in range(RING):
                step(0, k)
            with eng.Fori(1, SAMPLES // RING) as b:
                for k in range(RING):
                    step(b, k)
            for k in range(2):
                step(SAMPLES // RING, k)

        def within(b, k):
            return not isinstance(b, int) or 0 <= RING * b + k < SAMPLES

        def pairs(eng, pair):
            last_choice = SAMPLES - LEAD
            pair(0, True, False)
            with eng.Fori(1, LEAD) as p:
                pair(p, True, False)
            with eng.Fori(LEAD, last_choice) as p:
                pair(p, True, True)
            with eng.Fori(last_choice, SAMPLES) as p:
                pair(p, False, True)

        block = ctx.enter_context(nc.Block())

        @block.sync
        def _(sp):
            sp.dma_start(ids_s[:], ids.rearrange("(a n) -> a n", a=1)).then_inc(ids_loaded, 16)

            def load_sample(b, k):
                s = RING * b + k
                at_least(sp, xb_ready, 2 * (s - RING + 1))
                at_least(sp, xb_ready, 2 * (s - RING + 1))
                at_least(sp, xT_done, s - RING + 1)
                carried(sp, sp_ticks)
                sp.dma_start(xin[k][:], x[bass.ds(s, 1)].rearrange("a (t p) d -> p (a t) d", p=P)).then_inc(x_loaded[k], 16)
                at_least(sp, ynT_ready, 2 * (s - RING + 1))
                at_least(sp, ynT_ready, 2 * (s - RING + 1))
                at_least(sp, y_done, s - RING + 1)
                carried(sp, sp_ticks)
                pid = sp.value_load(ids_s[0:1, bass.ds(s, 1)], min_val=0, max_val=PROFILES - 1)
                sp.dma_start(pf[k][:], prof[bass.ds(pid, 1)].rearrange("a p n -> (a p) n")).then_inc(pf_loaded[k], 16)

            def store_parts(b, k):
                s = RING * b + k
                for l, (ready, buf) in enumerate(((hi_ready, hi), (lo_ready, lo))):
                    sp.wait_ge(ready, s + 1)
                    carried(sp, sp_ticks)
                    for c in range(CC):
                        dst = parts_d[bass.ds(b, 1), HPT * c:HPT * (c + 1), l, :, k * TOK:(k + 1) * TOK]
                        sp.dma_start(dst.rearrange("a h d t -> (a h) d t"),
                                     buf[k % 2][:, c, :].bitcast(F32)).then_inc(parts_stored[k % 2], 16)

            sp.wait_ge(ids_loaded, 16)
            load_sample(0, 0)
            for dst, src in ((ident_s, ident), (wm_s, wm), (bm_s, bm), (emb_s, emb)):
                sp.dma_start(dst[:], src).then_inc(head_consts, 16)
            load_sample(0, 1)
            load_sample(0, 2)
            for q in range(P // HD):
                sp.dma_start(w1_raw[HD * q:HD * (q + 1)], w1.rearrange("e d i -> d e i")).then_inc(tail_consts, 16)
            for dst, src in ((b1_s, b1), (w2_s, w2), (b2_s, b2), (wo_s, wo), (bo_s, bo), (sel_s, sel), (rank_s, rank)):
                sp.dma_start(dst[:], src).then_inc(tail_consts, 16)

            def step(b, k):
                ahead = (b, k + 3) if k == 0 else (b + 1, k - 1)
                if within(*ahead):
                    load_sample(*ahead)
                if within(*back(b, k, 1)):
                    store_parts(*back(b, k, 1))

            for k in range(RING):
                step(0, k)
            with sp.Fori(1, SAMPLES // RING - 1) as b:
                for k in range(RING):
                    step(b, k)
            for b, n in ((SAMPLES // RING - 1, RING), (SAMPLES // RING, 1)):
                for k in range(n):
                    step(b, k)

            def store_route(s):
                sp.wait_ge(routeT_ready, s + 1)
                carried(sp, sp_ticks)
                at_least(sp, route_stored, 16 * s)
                carried(sp, sp_ticks)
                dst = route_d[bass.ds(s // SPC, 1), :, bass.ds((s % SPC) * TOK, TOK)]
                sp.dma_start(dst.rearrange("a r t -> (a r) t"), routeT[:]).then_inc(route_stored, 16)

            def load_parts(u, k):
                at_least(sp, hidden_done, EXPERTS * (u - 1))
                at_least(sp, hidden_done, EXPERTS * (u - 1))
                at_least(sp, parts_loaded, 16 * u)
                carried(sp, sp_ticks)
                src = parts_d.rearrange("c h l d t -> (c h) (l d) t")[bass.ds(u, 1)]
                sp.dma_start(parts[k][:].bitcast(F32), src.to_broadcast([2, 2 * HD, CHUNK])).then_inc(parts_loaded, 16)

            def load_wb(u, k, stored):
                at_least(sp, weighted, 2 * GROUPS * (u - 1))
                at_least(sp, weighted, 2 * GROUPS * (u - 1))
                at_least(sp, wb_loaded, 16 * u)
                sp.wait_ge(route_stored, 16 * stored)
                carried(sp, sp_ticks)
                src = route_d.rearrange("c (h j g) t -> (c h) j (g t)", h=HEADS, g=GROUPS)[bass.ds(u, 1)]
                src = src.rearrange("a j n -> j a n").to_broadcast([GE, HD, GROUPS * CHUNK])
                sp.dma_start(wb[k][:].rearrange("p g t -> p (g t)"), src).then_inc(wb_loaded, 16)

            def store_mixed(u, k):
                sp.wait_ge(mixed_ready, u + 1)
                at_least(sp, mixed_stored, 16 * u)
                carried(sp, sp_ticks)
                dst = mixed_d.rearrange("c (h o) (q t) -> (c h) q o t", h=HEADS, q=HPT)[bass.ds(u, 1)]
                sp.dma_start(dst.rearrange("a q o t -> (a q) o t"), mixed[k][:]).then_inc(mixed_stored, 16)

            def load_back(s, stored):
                sp.wait_ge(mixed_stored, 16 * stored)
                carried(sp, sp_ticks)
                at_least(sp, proj_done, s)
                carried(sp, sp_ticks)
                src = mixed_d.rearrange("c (t r) n -> c r t n", r=P)[bass.ds(s // SPC, 1), :, :, bass.ds((s % SPC) * TOK, TOK)]
                sp.dma_start(mixT[:], src.rearrange("a r t n -> (a r) t n")).then_inc(mixT_loaded, 16)
                at_least(sp, fin_ready, s)
                at_least(sp, fin_ready, s)
                carried(sp, sp_ticks)
                sp.dma_start(xres[:], x[bass.ds(s, 1)].rearrange("a (t p) d -> p (a t) d", p=P)).then_inc(xres_loaded, 16)

            def store_out(s):
                sp.wait_ge(fin_ready, s + 1)
                carried(sp, sp_ticks)
                sp.dma_start(out[bass.ds(s, 1)].rearrange("a (t p) d -> p (a t) d", p=P), fin[:]).then_inc(out_stored, 16)

            for i in range(2):
                sp.wait_ge(parts_stored[i], 16 * 2 * CC * SAMPLES // 2)
            load_parts(0, 0)
            load_parts(1, 1)
            with sp.Fori(0, LEAD) as s:
                store_route(s)
            load_wb(0, 0, LEAD)

            def pair(p, choose, project, last=False):
                if project:
                    load_back(p - LEAD, 2 * p - 2)
                for k in range(2):
                    u = 2 * p + k
                    first = isinstance(p, int) and u == 0
                    if not first:
                        store_mixed(u - 1, 1 - k)
                    if not (last and k == 1):
                        if not first:
                            load_parts(u + 1, 1 - k)
                        load_wb(u + 1, 1 - k, p + LEAD if choose else SAMPLES)
                    if project and k == 0:
                        store_out(p - LEAD)
                if choose:
                    store_route(p + LEAD)

            pair(0, True, False)
            with sp.Fori(1, LEAD) as p:
                pair(p, True, False)
            with sp.Fori(LEAD, SAMPLES - LEAD) as p:
                pair(p, True, True)
            with sp.Fori(SAMPLES - LEAD, SAMPLES - 1) as p:
                pair(p, False, True)
            pair(SAMPLES - 1, False, True, last=True)
            store_mixed(UNITS - 1, 1)
            with sp.Fori(SAMPLES - LEAD, SAMPLES) as s:
                load_back(s, UNITS)
                store_out(s)
            sp.wait_ge(out_stored, 16 * SAMPLES)

        @block.gpsimd
        def _(pool):
            nc.gpsimd.memset(minus_half[:], -0.5).then_inc(half_set, 1)
            nc.gpsimd.memset(eps_s[:], EPS).then_inc(half_set, 1)
            pool.wait_ge(half_set, 2)

            def add_up_bias(b, k):
                s = RING * b + k
                pool.wait_ge(x_loaded[k], 16 * (b + 1))
                pool.wait_ge(pf_loaded[k], 16 * (b + 1))
                at_least(pool, y_ready, s - 1)
                for t in range(T2):
                    nc.gpsimd.tensor_tensor(xb[k % 2][:, t], xin[k][:, t], pf[k][:, UB:UB + D], ALU.add).then_inc(xb_ready, 1)

            def inverse_deviation(b, k):
                s = RING * b + k
                pool.wait_ge(mv_ready, 2 * s + 2)
                at_least(pool, rstd_step, 2 * s)
                nc.gpsimd.tensor_tensor(vareps[:], mv[k % 2][:, :, 1], eps_s[:], ALU.add).then_inc(rstd_step, 1)
                pool.wait_ge(rstd_step, 2 * s + 1)
                at_least(pool, yn_ready, 2 * (s - 1))
                nc.gpsimd.tensor_tensor(rstd[k % 2][:], vareps[:], minus_half[:], ALU.pow).then_inc(rstd_step, 1)

            def step(b, k):
                if within(b, k):
                    add_up_bias(b, k)
                    inverse_deviation(b, k)

            steps(pool, step)

            def sum_groups(u, k):
                pool.wait_ge(weighted, 2 * GROUPS * u + 4)
                at_least(pool, mixed_done, u - 1)
                nc.gpsimd.tensor_tensor(total[k][:], wout[:, 0], wout[:, 1], ALU.add).then_inc(summed, 1)
                for g in (2, 3):
                    pool.wait_ge(weighted, 2 * GROUPS * u + 2 * g + 2)
                    pool.wait_ge(summed, 3 * u + g - 1)
                    nc.gpsimd.tensor_tensor(total[k][:], total[k][:], wout[:, g], ALU.add).then_inc(summed, 1)

            def bias_residual(s):
                pool.wait_ge(xres_loaded, 16 * (s + 1))
                for t in range(T2):
                    nc.gpsimd.tensor_tensor(xres[:, t], xres[:, t], bo_s[:], ALU.add).then_inc(xres_biased, 1)

            def pair(p, choose, project):
                if project:
                    bias_residual(p - LEAD)
                for k in range(2):
                    sum_groups(2 * p + k, k)

            pool.wait_ge(tail_consts, 16 * 11)
            pairs(pool, pair)
            with pool.Fori(SAMPLES - LEAD, SAMPLES) as s:
                bias_residual(s)

        @block.scalar
        def _(act):
            def evacuate_xT(s):
                act.wait_ge(xT_done, s + 1)
                at_least(act, z_done, s)
                nc.scalar.activation(xT[:].rearrange("p c t -> p (c t)"), psum[:, B_XT], ACT.Identity).then_inc(xT_ready, 1)

            def evacuate_z(k, s):
                act.wait_ge(z_done, s + 1)
                at_least(act, y_done, s)
                nc.scalar.activation(zT[:], psum[:, B_Z, 0:TOK], ACT.Relu, bias=pf[k][:, DB:DB + 1]).then_inc(z_ready, 1)

            def scale_ynT(k, s):
                act.wait_ge(ynT_done, s + 1)
                at_least(act, hT_done, s)
                for c in range(CC):
                    nc.scalar.activation(ynT[:, c], psum[:, B_YNT, c * TOK:(c + 1) * TOK], ACT.Identity,
                                         bias=pf[k][:, LB + c:LB + c + 1], scale=pf[k][:, LG + c:LG + c + 1]).then_inc(ynT_ready, 1)

            def evacuate_hT(k, s):
                act.wait_ge(hT_done, s + 1)
                at_least(act, logits_done, s - 1)
                at_least(act, lo_ready, s - 1)
                for c in range(CC):
                    nc.scalar.activation(hT[k % 2][:, c], psum[:, B_HT, c * TOK:(c + 1) * TOK], ACT.Identity,
                                         bias=bm_s[:, c:c + 1]).then_inc(hT_ready, 1)

            def exponentials(s):
                act.wait_ge(ldiff_ready, s + 1)
                dst = prob[:, bass.ds(s, 1)].rearrange("p a n -> p (a n)")
                nc.scalar.activation(dst, ldiff[:], ACT.Exp).then_inc(prob_ready, 1)

            def step(b, k):
                s = RING * b + k
                one, two = back(b, k, 1), back(b, k, 2)
                if within(b, k):
                    evacuate_xT(s)
                if within(*one):
                    scale_ynT(one[1], s - 1)
                if within(*two):
                    exponentials(s - 2)
                if within(b, k):
                    evacuate_z(k, s)
                if within(*one):
                    evacuate_hT(one[1], s - 1)

            act.wait_ge(head_consts, 16 * 4)
            steps(act, step)
            act.wait_ge(tail_consts, 16 * 11)

            def pair(p, choose, project):
                for k in range(2):
                    u = 2 * p + k
                    for g in range(GROUPS):
                        for j in range(GE):
                            n, e = GE * g + j, GROUPS * j + g
                            act.wait_ge(hidden_done, EXPERTS * u + n + 1)
                            if j == 0:
                                at_least(act, expert_done, 2 * (GROUPS * u + g - 1))
                            nc.scalar.activation(hid[g % 2][:, j], psum[:, 2 * (n % 2):2 * (n % 2) + 2].rearrange("p b t -> p (b t)"),
                                                 ACT.Gelu, bias=b1_s[:, e:e + 1]).then_inc(gelu_done, 1)

            pairs(act, pair)

        @block.vector
        def _(dve):
            def normalise(k, s):
                dve.wait_ge(rstd_step, 2 * s + 2)
                at_least(dve, ynT_done, s)
                for t in range(T2):
                    nc.vector.tensor_scalar(yn[:, t], y[k % 2][:, t], mv[k % 2][:, t, 0:1], rstd[k % 2][:, t:t + 1],
                                            ALU.subtract, ALU.mult).then_inc(yn_ready, 1)

            def logit_differences(s):
                dve.wait_ge(logits_done, s + 1)
                grouped = psum[:, B_LOGIT, 0:T2 * HE].rearrange("p (g e) -> p g e", e=EXPERTS)
                at_least(dve, ldiff_ready, s)
                nc.vector.tensor_reduce(lmax[:], grouped, AX_X, ALU.max).then_inc(lmax_ready, 1)
                dve.wait_ge(lmax_ready, s + 1)
                at_least(dve, prob_ready, s)
                nc.vector.tensor_tensor(ldiff[:].rearrange("p (g e) -> p g e", e=EXPERTS), grouped,
                                        lmax[:].unsqueeze(2).to_broadcast([P, T2 * HEADS, EXPERTS]), ALU.subtract).then_inc(ldiff_ready, 1)

            def split_parts(b, k):
                s = RING * b + k
                dve.wait_ge(hT_ready, 2 * s + 2)
                at_least(dve, parts_stored[k % 2], 16 * 2 * CC * (2 * b + k // 2))
                nc.vector.tensor_copy(hi[k % 2][:], hT[k % 2][:]).then_inc(hi_ready, 1)
                dve.wait_ge(hi_ready, s + 1)
                nc.vector.tensor_tensor(lo[k % 2][:], hT[k % 2][:], hi[k % 2][:].bitcast(F32), ALU.subtract).then_inc(lo_ready, 1)

            def residual_and_statistics(k, s):
                dve.wait_ge(y_done, s + 1)
                dve.wait_ge(xb_ready, 2 * s + 2)
                nc.vector.tensor_tensor(y[k % 2][:].rearrange("p t d -> p (t d)"), psum[:, B_Y],
                                        xb[k % 2][:].rearrange("p t d -> p (t d)"), ALU.add).then_inc(y_ready, 1)
                dve.wait_ge(y_ready, s + 1)
                at_least(dve, mv_ready, 2 * s)
                for t in range(T2):
                    nc.vector.bn_stats(stats[:, t], y[k % 2][:, t]).then_inc(stats_ready, 1)
                dve.wait_ge(stats_ready, 2 * s + 2)
                carried(dve, dve_ticks)
                for t in range(T2):
                    nc.vector.bn_aggr(mv[k % 2][:, t], stats[:, t]).then_inc(mv_ready, 1)

            def step(b, k):
                s = RING * b + k
                one, two = back(b, k, 1), back(b, k, 2)
                if within(*one):
                    normalise(one[1], s - 1)
                if within(*two):
                    logit_differences(s - 2)
                if within(*one):
                    split_parts(*one)
                if within(b, k):
                    residual_and_statistics(k, s)

            steps(dve, step)

            dve.wait_ge(tail_consts, 16 * 11)
            nc.vector.tensor_copy(w1_s[:], w1_raw[:]).then_inc(w1_high, 1)
            dve.wait_ge(w1_high, 1)
            nc.vector.tensor_tensor(w1_s[P // 2:P], w1_raw[P // 2:P], w1_s[P // 2:P].bitcast(F32), ALU.subtract).then_inc(w1_split, 1)

            def by_head(t):
                return t[:].rearrange("p (g e) -> p g e", e=EXPERTS)

            def wide(t):
                return t[:].unsqueeze(2).to_broadcast([P, T2 * HEADS, EXPERTS])

            def choose_two(s, part):
                probs = prob[:, bass.ds(s, 1)].rearrange("p a n -> p (a n)")
                v = nc.vector
                done = [4 * part + (part > 0)]

                def own(ins):
                    done[0] += 1
                    ins.then_inc(choose_step, 1)
                    dve.wait_ge(choose_step, 17 * s + done[0])

                if part == 0:
                    dve.wait_ge(prob_ready, s + 1)
                    own(v.tensor_scalar(t_p[:], probs, 1.0, None, ALU.mult))
                    own(v.tensor_reduce(t_m[:], by_head(t_p), AX_X, ALU.max))
                    own(v.tensor_tensor(by_head(t_q), by_head(t_p), wide(t_m), ALU.is_equal))
                    own(v.tensor_tensor(t_s[:], t_q[:], rank_s[:], ALU.mult))
                    own(v.tensor_reduce(t_m[:], by_head(t_s), AX_X, ALU.max))
                elif part == 1:
                    own(v.tensor_tensor(by_head(t_one), by_head(t_s), wide(t_m), ALU.is_equal))
                    own(v.scalar_tensor_tensor(out=t_rest[:], in0=t_one[:], scalar=-2.0, in1=t_p[:], op0=ALU.mult, op1=ALU.add))
                    own(v.tensor_reduce(t_m[:], by_head(t_rest), AX_X, ALU.max))
                    own(v.tensor_tensor(by_head(t_q), by_head(t_rest), wide(t_m), ALU.is_equal))
                elif part == 2:
                    own(v.tensor_tensor(t_s[:], t_q[:], rank_s[:], ALU.mult))
                    own(v.tensor_reduce(t_m[:], by_head(t_s), AX_X, ALU.max))
                    own(v.tensor_tensor(by_head(t_two), by_head(t_s), wide(t_m), ALU.is_equal))
                    own(v.tensor_reduce(t_z[:], by_head(t_p), AX_X, ALU.add))
                else:
                    own(v.reciprocal(t_rz[:], t_z[:]))
                    own(v.tensor_tensor(t_two[:], t_one[:], t_two[:], ALU.add))
                    own(v.tensor_tensor(t_q[:], t_two[:], t_p[:], ALU.mult))
                    at_least(dve, routeT_done, s)
                    own(v.tensor_tensor(by_head(route), by_head(t_q), wide(t_rz), ALU.mult))

            def evacuate_routeT(s):
                dve.wait_ge(routeT_done, s + 1)
                at_least(dve, route_stored, 16 * s)
                nc.vector.tensor_copy(routeT[:], psum[:, B_AUX, 0:TOK]).then_inc(routeT_ready, 1)

            with dve.Fori(0, LEAD) as s:
                for part in range(4):
                    choose_two(s, part)
                evacuate_routeT(s)

            def weight(u, k, g):
                for h in range(2):
                    dve.wait_ge(expert_done, 2 * (GROUPS * u + g) + h + 1)
                    if h == 0 and g == 0:
                        dve.wait_ge(wb_loaded, 16 * (u + 1))
                    if h == 0:
                        at_least(dve, summed, 3 * (u - 1) + max(g, 1))
                    cols = slice(h * HALF, (h + 1) * HALF)
                    nc.vector.scalar_tensor_tensor(out=wout[:, g, cols], in0=psum[:, B_OUT + h], scalar=b2_s[:, g:g + 1],
                                                   in1=wb[k][:, g, cols], op0=ALU.add, op1=ALU.mult).then_inc(weighted, 1)

            def evacuate_mixed(u, k):
                dve.wait_ge(mixed_done, u + 1)
                at_least(dve, mixed_stored, 16 * (u - 1))
                nc.vector.tensor_copy(mixed[k][:], psum[:, B_MIX, 0:TOK]).then_inc(mixed_ready, 1)

            def finish_rows(s):
                dve.wait_ge(proj_done, s + 1)
                dve.wait_ge(xres_biased, 2 * s + 2)
                at_least(dve, out_stored, 16 * s)
                nc.vector.tensor_tensor(fin[:].rearrange("p t d -> p (t d)"), psum[:, B_AUX],
                                        xres[:].rearrange("p t d -> p (t d)"), ALU.add).then_inc(fin_ready, 1)

            def pair(p, choose, project):
                for k in range(2):
                    u = 2 * p + k
                    for g in range(GROUPS):
                        if g:
                            weight(u, k, g - 1)
                        elif not (isinstance(p, int) and u == 0):
                            weight(u - 1, 1 - k, GROUPS - 1)
                        if choose and k == 0:
                            choose_two(p + LEAD, g)
                        if project and (k, g) == (0, 1):
                            finish_rows(p - LEAD)
                        if choose and (k, g) == (1, 1):
                            evacuate_routeT(p + LEAD)
                        if g == 2 and not (isinstance(p, int) and u == 0):
                            evacuate_mixed(u - 1, 1 - k)

            pairs(dve, pair)
            weight(UNITS - 1, 1, GROUPS - 1)
            evacuate_mixed(UNITS - 1, 1)
            with dve.Fori(SAMPLES - LEAD, SAMPLES) as s:
                finish_rows(s)

        @block.tensor
        def _(pe):
            def router(k, s):
                pe.wait_ge(hT_ready, 2 * s + 2)
                at_least(pe, ldiff_ready, s)
                for t in range(T2):
                    for c in range(CC):
                        at = t * HE + c * HPT * EXPERTS
                        last = nc.tensor.matmul(psum[:, B_LOGIT, at:at + HPT * EXPERTS], hT[k % 2][:, c, t * P:(t + 1) * P],
                                                emb_s[:], start=True, stop=True)
                last.then_inc(logits_done, 1)

            def turn_x(b, k, s):
                pe.wait_ge(x_loaded[k], 16 * (b + 1))
                at_least(pe, xT_ready, s)
                for t in range(T2):
                    for c in range(CC):
                        at = c * TOK + t * P
                        last = nc.tensor.transpose(psum[:, B_XT, at:at + P], xin[k][:, t, c * P:(c + 1) * P], ident_s[:])
                last.then_inc(xT_done, 1)

            def turn_yn(s):
                pe.wait_ge(yn_ready, 2 * s + 2)
                at_least(pe, ynT_ready, 2 * s)
                for t in range(T2):
                    for c in range(CC):
                        at = c * TOK + t * P
                        last = nc.tensor.transpose(psum[:, B_YNT, at:at + P], yn[:, t, c * P:(c + 1) * P], ident_s[:])
                last.then_inc(ynT_done, 1)

            def down(b, k, s):
                pe.wait_ge(xT_ready, s + 1)
                pe.wait_ge(pf_loaded[k], 16 * (b + 1))
                at_least(pe, z_ready, s)
                for c in range(CC):
                    last = nc.tensor.matmul(psum[:, B_Z, 0:TOK], pf[k][:, DOWN + c * NECK:DOWN + (c + 1) * NECK], xT[:, c],
                                            start=(c == 0), stop=(c == CC - 1))
                last.then_inc(z_done, 1)

            def project_heads(s):
                pe.wait_ge(ynT_ready, 2 * s + 2)
                at_least(pe, hT_ready, 2 * s)
                for o in range(CC):
                    for c in range(CC):
                        last = nc.tensor.matmul(psum[:, B_HT, o * TOK:(o + 1) * TOK], wm_s[:, c, o * P:(o + 1) * P], ynT[:, c],
                                                start=(c == 0), stop=(c == CC - 1))
                last.then_inc(hT_done, 1)

            def up(k, s):
                pe.wait_ge(z_ready, s + 1)
                at_least(pe, y_ready, s)
                for t in range(T2):
                    last = nc.tensor.matmul(psum[:, B_Y, t * D:(t + 1) * D], zT[:, t * P:(t + 1) * P], pf[k][:, UP:UP + D],
                                            start=True, stop=True)
                last.then_inc(y_done, 1)

            def step(b, k):
                s = RING * b + k
                one, two = back(b, k, 1), back(b, k, 2)
                if within(*two):
                    router(two[1], s - 2)
                if within(b, k):
                    turn_x(b, k, s)
                if within(*one):
                    turn_yn(s - 1)
                if within(b, k):
                    down(b, k, s)
                if within(*one):
                    project_heads(s - 1)
                if within(b, k):
                    up(k, s)

            pe.wait_ge(head_consts, 16 * 4)
            steps(pe, step)

            def turn_route(s):
                pe.wait_ge(choose_step, 17 * (s + 1))
                at_least(pe, routeT_ready, s)
                for t in range(T2):
                    last = nc.tensor.transpose(psum[:, B_AUX, t * P:(t + 1) * P], route[:, t * HE:(t + 1) * HE], ident_s[:])
                last.then_inc(routeT_done, 1)

            with pe.Fori(0, LEAD) as s:
                turn_route(s)
            pe.wait_ge(w1_split, 1)
            pe.wait_ge(prob_ready, SAMPLES)
            pe.wait_ge(tail_consts, 16 * 11)

            def hidden(u, k, n):
                e = GROUPS * (n % GE) + n // GE
                at_least(pe, gelu_done, EXPERTS * u + n - 1)
                for h in range(2):
                    last = nc.tensor.matmul(psum[:, 2 * (n % 2) + h], w1_s[:, e], parts[k][:, h * HALF:(h + 1) * HALF], start=True, stop=True)
                last.then_inc(hidden_done, 1)

            def experts(u, g, h):
                if h == 0:
                    pe.wait_ge(gelu_done, EXPERTS * u + GE * (g + 1))
                at_least(pe, weighted, 2 * (GROUPS * u + g) + h - 1)
                for j in range(GE):
                    last = nc.tensor.matmul(psum[HD * j:HD * (j + 1), B_OUT + h], w2_s[:, GROUPS * j + g], hid[g % 2][:, j, h * HALF:(h + 1) * HALF],
                                            start=True, stop=True)
                last.then_inc(expert_done, 1)

            def mix(u, k):
                pe.wait_ge(summed, 3 * u + 3)
                at_least(pe, mixed_ready, u)
                for q in range(HPT):
                    last = nc.tensor.matmul(psum[HD * q:HD * (q + 1), B_MIX, 0:TOK], sel_s[:], total[k][:, q * TOK:(q + 1) * TOK],
                                            start=True, stop=True)
                last.then_inc(mixed_done, 1)

            def project_out(s, t):
                if t == 0:
                    pe.wait_ge(mixT_loaded, 16 * (s + 1))
                    at_least(pe, fin_ready, s)
                for c in range(CC):
                    last = nc.tensor.matmul(psum[:, B_AUX, t * D:(t + 1) * D], mixT[:, c, t * P:(t + 1) * P], wo_s[:, c],
                                            start=(c == 0), stop=(c == CC - 1))
                if t == T2 - 1:
                    last.then_inc(proj_done, 1)

            def pair(p, choose, project):
                for k in range(2):
                    u = 2 * p + k
                    first = isinstance(p, int) and u == 0
                    pe.wait_ge(parts_loaded, 16 * (u + 1))
                    for g in range(GROUPS):
                        before = None if first and g == 0 else (u, g - 1) if g else (u - 1, GROUPS - 1)
                        for j in range(GE):
                            hidden(u, k, GE * g + j)
                            if j < 2 and before:
                                experts(*before, j)
                            if project and (k, g) == (0, 1) and j >= 2:
                                if j == 2:
                                    pe.wait_ge(routeT_ready, LEAD + p if choose else SAMPLES)
                                project_out(p - LEAD, j - 2)
                            if choose and (k, g, j) == (1, 1, 2):
                                if project:
                                    pe.wait_ge(fin_ready, p - LEAD + 1)
                                turn_route(p + LEAD)
                            if (g, j) == (2, 2) and not first:
                                mix(u - 1, 1 - k)

            pairs(pe, pair)
            for h in range(2):
                experts(UNITS - 1, GROUPS - 1, h)
            mix(UNITS - 1, 1)
            with pe.Fori(SAMPLES - LEAD, SAMPLES) as s:
                for t in range(T2):
                    project_out(s, t)


def kernel(x, itok_B_0_6, L0_cond_down_w, L0_cond_down_b, L0_cond_up_w, L0_cond_up_b, L0_cond_ln_g, L0_cond_ln_b,
           L0_ffn_Wm, L0_ffn_bm, L0_ffn_expert_emb, L0_ffn_W1, L0_ffn_b1, L0_ffn_W2, L0_ffn_b2, L0_ffn_Wo, L0_ffn_bo):
    import numpy as np
    import concourse.bacc as bacc
    from concourse.bass_utils import run_bass_kernel_spmd

    def tiles(a):
        return np.asarray(a).reshape(-1, P, a.shape[-1]).transpose(1, 0, 2)

    def columns(a):
        return np.asarray(a).reshape(-1, P).T

    prof = np.zeros((PROFILES, P, PW), np.float32)
    for i in range(PROFILES):
        prof[i, :, DOWN:UP] = tiles(L0_cond_down_w[i]).reshape(P, -1)
        prof[i, :, UP:DB] = L0_cond_up_w[i]
        prof[i, :, DB] = L0_cond_down_b[i]
        prof[i, :, LG:LB] = columns(L0_cond_ln_g[i])
        prof[i, :, LB:UB] = columns(L0_cond_ln_b[i])
        prof[i, :, UB:] = L0_cond_up_b[i]
    emb = np.zeros((P, HPT * EXPERTS), np.float32)
    for h in range(HPT):
        emb[HD * h:HD * (h + 1), EXPERTS * h:EXPERTS * (h + 1)] = L0_ffn_expert_emb
    arrays = {
        "x": x, "ids": itok_B_0_6, "prof": prof, "wm": tiles(L0_ffn_Wm), "bm": columns(L0_ffn_bm), "emb": emb,
        "w1": L0_ffn_W1, "b1": np.asarray(L0_ffn_b1).T, "w2": np.asarray(L0_ffn_W2).transpose(1, 0, 2),
        "b2": np.asarray(L0_ffn_b2).reshape(GE, GROUPS, HD).transpose(0, 2, 1).reshape(P, GROUPS),
        "wo": tiles(L0_ffn_Wo), "bo": np.broadcast_to(np.asarray(L0_ffn_bo), (P, D)),
        "ident": np.eye(P, dtype=np.float32), "sel": np.tile(np.eye(HD, dtype=np.float32), (GE, 1)),
        "rank": np.tile(np.arange(EXPERTS, 0, -1, dtype=np.float32), (P, TOK // EXPERTS)),
    }
    nc = bacc.Bacc("TRN2", target_bir_lowering=False, num_devices=1)
    held, args = {}, []
    for name, a in arrays.items():
        a = np.ascontiguousarray(a)
        held[f"in_{name}"] = a
        args.append(nc.dram_tensor(f"in_{name}", a.shape, mybir.dt.from_np(a.dtype), kind="ExternalInput").ap())
    out = nc.dram_tensor("out_rows", (SAMPLES, TOK, D), F32, kind="ExternalOutput").ap()
    build(nc, *args, out)
    return run_bass_kernel_spmd(nc, [held], core_ids=[0]).results[0]["out_rows"]
```

```python
from contextlib import ExitStack

import concourse.bass as bass
from concourse import mybir

F32 = mybir.dt.float32
F32R = mybir.dt.float32r
I32 = mybir.dt.int32
ALU = mybir.AluOpType
ACT = mybir.ActivationFunctionType
AX_X = mybir.AxisListType.X

P = 128
SAMPLES, TOK, D = 16, 256, 256
T2 = TOK // P
CC = D // P
PROFILES, NECK = 8, 128
HEADS, HD = 8, 32
EXPERTS, HID = 16, 128
EPS = 1e-5
CHUNK = 1024
SPC = CHUNK // TOK
CHUNKS = SAMPLES // SPC
UNITS = CHUNKS * HEADS
HALF = 512
GROUPS, GE = 4, 4
HPT = P // HD
HE = HEADS * EXPERTS
RING = 4
LEAD = 6
LAG = SPC
TAIL = 3
START = 1
CHOOSE = 14

DOWN, UP, DB, LG, LB, UB = 0, 256, 512, 513, 515, 517
PW = UB + D


def at_least(eng, sem, value):
    if not isinstance(value, int) or value > 0:
        eng.wait_ge(sem, value)


def from_start(eng, sem, value):
    if not isinstance(value, int) or value > 0:
        eng.wait_ge(sem, value + START)


def carried(eng, ticks):
    eng.sem_inc(ticks, 1)


def build(nc, x, ids, prof, wm, bm, emb, w1, b1, w2, b2, wo, bo, ident, sel, rank, out):
    with ExitStack() as ctx:
        def sb(name, shape, dt=F32):
            return ctx.enter_context(nc.sbuf_tensor(name, shape, dt))

        def sem(name):
            return ctx.enter_context(nc.semaphore(name))

        parts_d = nc.dram_tensor("parts_scratch", (CHUNKS, HEADS, 2, HD, CHUNK), F32, kind="Internal").ap()
        route_d = nc.dram_tensor("route_scratch", (CHUNKS, HE, CHUNK), F32, kind="Internal").ap()
        mixed_d = nc.dram_tensor("mixed_scratch", (CHUNKS, HEADS * HD, CHUNK), F32, kind="Internal").ap()

        psum = ctx.enter_context(nc.psum_tensor("psum", [P, 8, HALF], F32))

        ids_s = sb("ids_s", [1, SAMPLES], I32)
        wm_s = sb("wm_s", [P, CC, D])
        bm_s = sb("bm_s", [P, CC])
        emb_s = sb("emb_s", [P, HPT * EXPERTS])
        w1_s = sb("w1_s", [P, EXPERTS, HID], F32R)
        b1_s = sb("b1_s", [P, EXPERTS])
        w2_s = sb("w2_s", [P, EXPERTS, HD])
        b2_s = sb("b2_s", [P, GROUPS])
        wo_s = sb("wo_s", [P, CC, D])
        bo_s = sb("bo_s", [P, D])
        ident_s = sb("ident_s", [P, P])
        sel_s = sb("sel_s", [P, HD])
        rank_s = sb("rank_s", [P, TOK])
        minus_half = sb("minus_half", [P, T2])
        eps_s = sb("eps_s", [P, T2])

        xin = [sb(f"xin{i}", [P, T2, D]) for i in range(RING)]
        pf = [sb(f"pf{i}", [P, PW]) for i in range(RING)]
        xb = [sb(f"xb{i}", [P, T2, D]) for i in range(2)]
        zT = sb("zT", [P, TOK])
        y = [sb(f"y{i}", [P, T2, D]) for i in range(2)]
        stats = sb("stats", [P, T2, 6])
        mv = [sb(f"mv{i}", [P, T2, 2]) for i in range(2)]
        vareps = sb("vareps", [P, T2])
        rstd = [sb(f"rstd{i}", [P, T2]) for i in range(2)]
        yn = sb("yn", [P, T2, D])
        mix_last = sb("mix_last", [P, CC, CHUNK])
        hT = [mix_last[:, i, 0:HALF].rearrange("p (c t) -> p c t", c=CC) for i in range(2)]
        xT, ynT = (mix_last[:, i, HALF:CHUNK].rearrange("p (c t) -> p c t", c=CC) for i in range(2))
        hi = [sb(f"hi{i}", [P, CC, TOK], F32R) for i in range(2)]
        lo = [sb(f"lo{i}", [P, CC, TOK], F32R) for i in range(2)]
        lmax = sb("lmax", [P, T2 * HEADS])
        ldiff = sb("ldiff", [P, SAMPLES, T2 * HE])
        prob = sb("prob", [P, SAMPLES, T2 * HE])

        t_q = sb("t_q", [P, T2 * HE])
        t_s = sb("t_s", [P, T2 * HE])
        t_one = sb("t_one", [P, T2 * HE])
        t_rest = sb("t_rest", [P, T2 * HE])
        t_two = sb("t_two", [P, T2 * HE])
        t_m = sb("t_m", [P, T2 * HEADS])
        t_z = sb("t_z", [P, T2 * HEADS])
        t_rz = sb("t_rz", [P, T2 * HEADS])
        route = sb("route", [P, T2 * HE])
        routeT = sb("routeT", [P, TOK])

        parts = [sb(f"parts{i}", [P, CHUNK], F32R) for i in range(2)]
        wb = [sb(f"wb{i}", [P, GROUPS, CHUNK]) for i in range(2)]
        hid = [sb(f"hid{i}", [P, GE, CHUNK]) for i in range(2)]
        w1_raw = hid[0][:, 0:2].rearrange("p a (e i) -> p (a e) i", i=HID)
        wout = sb("wout", [P, GROUPS, CHUNK])
        total = [sb(f"total{i}", [P, CHUNK]) for i in range(2)]
        mixed = [sb(f"mixed{i}", [P, TOK]) for i in range(2)]
        mixT = sb("mixT", [P, CC, TOK])
        xres = sb("xres", [P, T2, D])
        fin = sb("fin", [P, T2, D])
        xres_last, fin_last = xin, xb + y

        ids_loaded, head_consts, tail_consts = sem("ids_loaded"), sem("head_consts"), sem("tail_consts")
        x_loaded = [sem(f"x_loaded{i}") for i in range(RING)]
        pf_loaded = [sem(f"pf_loaded{i}") for i in range(RING)]
        parts_stored = [sem(f"parts_stored{i}") for i in range(2)]
        route_stored, mixed_stored, out_stored = sem("route_stored"), sem("mixed_stored"), sem("out_stored")
        parts_loaded, wb_loaded = sem("parts_loaded"), sem("wb_loaded")
        mixT_loaded, xres_loaded = sem("mixT_loaded"), sem("xres_loaded")
        xres_last_loaded = sem("xres_last_loaded")
        early_loaded = sem("early_loaded")
        last_loaded = [sem(f"last_loaded{i}") for i in range(SPC)]
        half_set = sem("half_set")
        sp_ticks, dve_ticks = sem("sp_ticks"), sem("dve_ticks")
        w1_high, w1_split = sem("w1_high"), sem("w1_split")
        xb_ready = sem("xb_ready")
        xT_done, xT_ready = sem("xT_done"), sem("xT_ready")
        z_done, z_ready = sem("z_done"), sem("z_ready")
        y_done, y_ready = sem("y_done"), sem("y_ready")
        stats_ready, mv_ready = sem("stats_ready"), sem("mv_ready")
        rstd_step = sem("rstd_step")
        yn_ready = sem("yn_ready")
        ynT_done, ynT_ready = sem("ynT_done"), sem("ynT_ready")
        hT_done, hT_ready = sem("hT_done"), sem("hT_ready")
        hi_ready, lo_ready = sem("hi_ready"), sem("lo_ready")
        logits_done, lmax_ready, ldiff_ready = sem("logits_done"), sem("lmax_ready"), sem("ldiff_ready")
        prob_ready = sem("prob_ready")
        choose_step = sem("choose_step")
        routeT_done, routeT_ready = sem("routeT_done"), sem("routeT_ready")
        hidden_done = sem("hidden_done")
        gelu_done = sem("gelu_done")
        expert_done = sem("expert_done")
        weighted = sem("weighted")
        summed = sem("summed")
        mixed_done, mixed_ready = sem("mixed_done"), sem("mixed_ready")
        proj_done, xres_biased, fin_ready = sem("proj_done"), sem("xres_biased"), sem("fin_ready")

        B_LOGIT, B_XT, B_YNT, B_Z, B_HT, B_Y = range(6)
        B_OUT, B_AUX = 6, 7

        def back(b, k, lag):
            return b + (k - lag) // RING, (k - lag) % RING

        def steps(step, eng, between=None):
            for k in range(RING):
                step(0, k)
            if between:
                between()
            with eng.Fori(1, SAMPLES // RING) as b:
                for k in range(RING):
                    step(b, k)
            for k in range(TAIL):
                step(SAMPLES // RING, k)

        def within(b, k):
            return not isinstance(b, int) or 0 <= RING * b + k < SAMPLES

        def choosing(b):
            return not isinstance(b, int)

        def pairs(eng, pair):
            pair(0, True, False)
            with eng.Fori(1, LAG) as p:
                pair(p, True, False)
            with eng.Fori(LAG, SAMPLES - LEAD) as p:
                pair(p, True, True)
            with eng.Fori(SAMPLES - LEAD, SAMPLES) as p:
                pair(p, False, True)

        def hidden_banks(k, n):
            i = (k + n) % 3
            return psum[:, 2 * i:2 * i + 2].rearrange("p b t -> p (b t)")

        block = ctx.enter_context(nc.Block())

        @block.sync
        def _(sp):
            for begun in (route_stored, mixed_stored, out_stored, *parts_stored):
                sp.sem_inc(begun, START)
            sp.dma_start(ids_s[:], ids.rearrange("(a n) -> a n", a=1)).then_inc(ids_loaded, 16)

            def load_sample(b, k):
                s = RING * b + k
                at_least(sp, xb_ready, 2 * (s - RING + 1))
                at_least(sp, xT_done, s - RING + 1)
                carried(sp, sp_ticks)
                sp.dma_start(xin[k][:], x[bass.ds(s, 1)].rearrange("a (t p) d -> p (a t) d", p=P)).then_inc(x_loaded[k], 16)
                at_least(sp, ynT_ready, 2 * (s - RING + 1))
                at_least(sp, y_done, s - RING + 1)
                carried(sp, sp_ticks)
                pid = sp.value_load(ids_s[0:1, bass.ds(s, 1)], min_val=0, max_val=PROFILES - 1)
                sp.dma_start(pf[k][:], prof[bass.ds(pid, 1)].rearrange("a p n -> (a p) n")).then_inc(pf_loaded[k], 16)

            def store_parts(b, k):
                s = RING * b + k
                for l, (ready, n, buf) in enumerate(((hi_ready, 2 * s + 2, hi), (lo_ready, s + 1, lo))):
                    sp.wait_ge(ready, n)
                    carried(sp, sp_ticks)
                    for c in range(CC):
                        dst = parts_d[bass.ds(b, 1), HPT * c:HPT * (c + 1), l, :, k * TOK:(k + 1) * TOK]
                        sp.dma_start(dst.rearrange("a h d t -> (a h) d t"),
                                     buf[k % 2][:, c, :].bitcast(F32)).then_inc(parts_stored[k % 2], 16)

            sp.wait_ge(ids_loaded, 16)
            load_sample(0, 0)
            for dst, src in ((ident_s, ident), (wm_s, wm), (bm_s, bm), (emb_s, emb)):
                sp.dma_start(dst[:], src).then_inc(head_consts, 16)
            load_sample(0, 1)
            for q in range(P // HD):
                sp.dma_start(w1_raw[HD * q:HD * (q + 1)], w1.rearrange("e d i -> d e i")).then_inc(tail_consts, 16)
            for dst, src in ((b1_s, b1), (w2_s, w2), (b2_s, b2), (wo_s, wo), (bo_s, bo), (sel_s, sel), (rank_s, rank)):
                sp.dma_start(dst[:], src).then_inc(tail_consts, 16)

            def step(b, k):
                ahead = (b, k + 2) if k < 2 else (b + 1, k - 2)
                if within(*ahead):
                    load_sample(*ahead)
                if within(*back(b, k, 3)):
                    store_parts(*back(b, k, 3))
                if choosing(b) and k >= 2:
                    store_route(2 * b + k - 4)

            def store_route(s):
                from_start(sp, routeT_ready, s + 1)
                carried(sp, sp_ticks)
                from_start(sp, route_stored, 16 * s)
                carried(sp, sp_ticks)
                dst = route_d[bass.ds(s // SPC, 1), :, bass.ds((s % SPC) * TOK, TOK)]
                sp.dma_start(dst.rearrange("a r t -> (a r) t"), routeT[:]).then_inc(route_stored, 16)

            def load_parts(u, k):
                at_least(sp, hidden_done, EXPERTS * (u - 1))
                at_least(sp, parts_loaded, 16 * u)
                carried(sp, sp_ticks)
                src = parts_d.rearrange("c h l d t -> (c h) (l d) t")[bass.ds(u, 1)]
                sp.dma_start(parts[k][:].bitcast(F32), src.to_broadcast([2, 2 * HD, CHUNK])).then_inc(parts_loaded, 16)

            def load_wb(u, k, stored):
                at_least(sp, weighted, 2 * GROUPS * (u - 1))
                at_least(sp, wb_loaded, 16 * u)
                from_start(sp, route_stored, 16 * stored)
                carried(sp, sp_ticks)
                src = route_d.rearrange("c (h j g) t -> (c h) j (g t)", h=HEADS, g=GROUPS)[bass.ds(u, 1)]
                src = src.rearrange("a j n -> j a n").to_broadcast([GE, HD, GROUPS * CHUNK])
                sp.dma_start(wb[k][:].rearrange("p g t -> p (g t)"), src).then_inc(wb_loaded, 16)

            def store_mixed(u, k):
                sp.wait_ge(mixed_ready, u + 1)
                carried(sp, sp_ticks)
                from_start(sp, mixed_stored, 16 * u)
                carried(sp, sp_ticks)
                dst = mixed_d.rearrange("c (h o) (q t) -> (c h) q o t", h=HEADS, q=HPT)[bass.ds(u, 1)]
                sp.dma_start(dst.rearrange("a q o t -> (a q) o t"), mixed[k][:]).then_inc(mixed_stored, 16)

            def load_back(s, stored):
                from_start(sp, mixed_stored, 16 * stored)
                carried(sp, sp_ticks)
                from_start(sp, proj_done, s)
                carried(sp, sp_ticks)
                src = mixed_d.rearrange("c (t r) n -> c r t n", r=P)[bass.ds(s // SPC, 1), :, :, bass.ds((s % SPC) * TOK, TOK)]
                sp.dma_start(mixT[:], src.rearrange("a r t n -> (a r) t n")).then_inc(mixT_loaded, 16)
                from_start(sp, fin_ready, s)
                carried(sp, sp_ticks)
                sp.dma_start(xres[:], x[bass.ds(s, 1)].rearrange("a (t p) d -> p (a t) d", p=P)).then_inc(xres_loaded, 16)

            def store_out(s):
                from_start(sp, fin_ready, s + 1)
                carried(sp, sp_ticks)
                sp.dma_start(out[bass.ds(s, 1)].rearrange("a (t p) d -> p (a t) d", p=P), fin[:]).then_inc(out_stored, 16)

            def last_block(b):
                for k in range(RING):
                    if k < 2:
                        load_sample(b, k + 2)
                    store_parts(*back(b, k, 3))
                    if k >= 2:
                        store_route(2 * b + k - 4)

            for k in range(RING):
                step(0, k)
            with sp.Fori(1, SAMPLES // RING - 1) as b:
                for k in range(RING):
                    step(b, k)
            last_block(SAMPLES // RING - 1)
            load_parts(0, 0)
            load_parts(1, 1)
            load_wb(0, 0, LEAD)
            for k in range(TAIL):
                step(SAMPLES // RING, k)
            for i in range(2):
                from_start(sp, parts_stored[i], 16 * 2 * CC * SAMPLES // 2)

            def pair(p, choose, project, last=False):
                chosen = p + LEAD if choose else SAMPLES
                first = isinstance(p, int) and p == 0
                if not first:
                    store_mixed(2 * p - 2, 0)
                    load_parts(2 * p + 1, 1)
                load_wb(2 * p + 1, 1, chosen)
                if not first:
                    store_mixed(2 * p - 1, 1)
                if project:
                    load_back(p - LAG, 2 * p)
                if not last:
                    load_parts(2 * p + 2, 0)
                if choose:
                    store_route(p + LEAD)
                if not last:
                    load_wb(2 * p + 2, 0, chosen)
                if project:
                    store_out(p - LAG)

            pair(0, True, False)
            with sp.Fori(1, LAG) as p:
                pair(p, True, False)
            with sp.Fori(LAG, SAMPLES - LEAD) as p:
                pair(p, True, True)
            with sp.Fori(SAMPLES - LEAD, SAMPLES - 1) as p:
                pair(p, False, True)
            for i in range(SPC):
                sp.dma_start(xres_last[i][:], x[SAMPLES - SPC + i].rearrange("(t p) d -> p t d", p=P)).then_inc(xres_last_loaded, 16)
            pair(SAMPLES - 1, False, True, last=True)
            store_mixed(UNITS - 2, 0)
            from_start(sp, mixed_stored, 16 * (UNITS - 1))
            rows = mixed_d[CHUNKS - 1].rearrange("(t r) n -> t r n", r=P)
            sp.dma_start(mix_last[:, 0], rows[0]).then_inc(early_loaded, 16)
            sp.dma_start(mix_last[0:P - HD, 1], rows[1, 0:P - HD]).then_inc(early_loaded, 16)
            sp.wait_ge(mixed_ready, UNITS)
            for i in range(SPC):
                sp.dma_start(mix_last[P - HD:P, 1, i * TOK:(i + 1) * TOK], mixed[1][HD * i:HD * (i + 1)]).then_inc(last_loaded[i], 16)
            for i in range(SPC):
                from_start(sp, fin_ready, SAMPLES - SPC + i + 1)
                sp.dma_start(out[SAMPLES - SPC + i].rearrange("(t p) d -> p t d", p=P), fin_last[i][:]).then_inc(out_stored, 16)
            from_start(sp, out_stored, 16 * SAMPLES)

        @block.gpsimd
        def _(pool):
            nc.gpsimd.memset(minus_half[:], -0.5).then_inc(half_set, 1)
            nc.gpsimd.memset(eps_s[:], EPS).then_inc(half_set, 1)
            pool.wait_ge(half_set, 2)

            def add_up_bias(b, k):
                s = RING * b + k
                pool.wait_ge(x_loaded[k], 16 * (b + 1))
                pool.wait_ge(pf_loaded[k], 16 * (b + 1))
                at_least(pool, y_ready, s - 1)
                for t in range(T2):
                    nc.gpsimd.tensor_tensor(xb[k % 2][:, t], xin[k][:, t], pf[k][:, UB:UB + D], ALU.add).then_inc(xb_ready, 1)

            def inverse_deviation(b, k):
                s = RING * b + k
                pool.wait_ge(mv_ready, 2 * s + 2)
                at_least(pool, rstd_step, 2 * s)
                nc.gpsimd.tensor_tensor(vareps[:], mv[k % 2][:, :, 1], eps_s[:], ALU.add).then_inc(rstd_step, 1)
                pool.wait_ge(rstd_step, 2 * s + 1)
                at_least(pool, yn_ready, 2 * (s - 1))
                nc.gpsimd.tensor_tensor(rstd[k % 2][:], vareps[:], minus_half[:], ALU.pow).then_inc(rstd_step, 1)

            def step(b, k):
                if within(b, k):
                    add_up_bias(b, k)
                if within(*back(b, k, 1)):
                    inverse_deviation(*back(b, k, 1))

            steps(step, pool)

            def sum_groups(u, k):
                pool.wait_ge(weighted, 2 * GROUPS * u + 4)
                at_least(pool, mixed_done, u - 1)
                nc.gpsimd.tensor_tensor(total[k][:], wout[:, 0], wout[:, 1], ALU.add).then_inc(summed, 1)
                for g in (2, 3):
                    pool.wait_ge(weighted, 2 * GROUPS * u + 2 * g + 2)
                    pool.wait_ge(summed, 3 * u + g - 1)
                    nc.gpsimd.tensor_tensor(total[k][:], total[k][:], wout[:, g], ALU.add).then_inc(summed, 1)

            def bias_residual(s, rows):
                for t in range(T2):
                    nc.gpsimd.tensor_tensor(rows[:, t], rows[:, t], bo_s[:], ALU.add).then_inc(xres_biased, 1)

            def pair(p, choose, project):
                sum_groups(2 * p, 0)
                if project:
                    pool.wait_ge(xres_loaded, 16 * (p - LAG + 1))
                    bias_residual(p - LAG, xres)
                sum_groups(2 * p + 1, 1)

            pool.wait_ge(tail_consts, 16 * 11)
            pairs(pool, pair)
            pool.wait_ge(xres_last_loaded, 16 * SPC)
            for i in range(SPC):
                bias_residual(SAMPLES - SPC + i, xres_last[i])

        @block.scalar
        def _(act):
            def evacuate_xT(s):
                act.wait_ge(xT_done, s + 1)
                at_least(act, z_done, s)
                nc.scalar.activation(xT.rearrange("p c t -> p (c t)"), psum[:, B_XT], ACT.Identity).then_inc(xT_ready, 1)

            def evacuate_z(k, s):
                act.wait_ge(z_done, s + 1)
                at_least(act, y_done, s)
                nc.scalar.activation(zT[:], psum[:, B_Z, 0:TOK], ACT.Relu, bias=pf[k][:, DB:DB + 1]).then_inc(z_ready, 1)

            def scale_ynT(k, s):
                act.wait_ge(ynT_done, s + 1)
                at_least(act, hT_done, s)
                for c in range(CC):
                    nc.scalar.activation(ynT[:, c], psum[:, B_YNT, c * TOK:(c + 1) * TOK], ACT.Identity,
                                         bias=pf[k][:, LB + c:LB + c + 1], scale=pf[k][:, LG + c:LG + c + 1]).then_inc(ynT_ready, 1)

            def evacuate_hT(b, k):
                s = RING * b + k
                act.wait_ge(hT_done, s + 1)
                at_least(act, logits_done, s - 1)
                at_least(act, lo_ready, s - 1)
                from_start(act, parts_stored[k % 2], 16 * 2 * CC * (2 * b + k // 2))
                for c in range(CC):
                    nc.scalar.activation(hT[k % 2][:, c], psum[:, B_HT, c * TOK:(c + 1) * TOK], ACT.Identity,
                                         bias=bm_s[:, c:c + 1]).then_inc(hT_ready, 1)
                    nc.scalar.activation(hi[k % 2][:, c], psum[:, B_HT, c * TOK:(c + 1) * TOK], ACT.Identity,
                                         bias=bm_s[:, c:c + 1]).then_inc(hi_ready, 1)

            def exponentials(s):
                act.wait_ge(ldiff_ready, s + 1)
                dst = prob[:, bass.ds(s, 1)].rearrange("p a n -> p (a n)")
                src = ldiff[:, bass.ds(s, 1)].rearrange("p a n -> p (a n)")
                nc.scalar.activation(dst, src, ACT.Exp).then_inc(prob_ready, 1)

            def step(b, k):
                s = RING * b + k
                two, three = back(b, k, 2), back(b, k, 3)
                if within(b, k):
                    evacuate_xT(s)
                if within(*two):
                    scale_ynT(two[1], s - 2)
                if within(b, k):
                    evacuate_z(k, s)
                if within(*three):
                    exponentials(s - 3)
                if within(*two):
                    evacuate_hT(*two)

            act.wait_ge(head_consts, 16 * 4)
            steps(step, act)
            act.wait_ge(tail_consts, 16 * 11)

            def pair(p, choose, project):
                for k in range(2):
                    u = 2 * p + k
                    for g in range(GROUPS):
                        for j in range(GE):
                            n, e = GE * g + j, GROUPS * j + g
                            act.wait_ge(hidden_done, EXPERTS * u + n + 1)
                            if j == 0:
                                at_least(act, expert_done, 2 * (GROUPS * u + g - 1))
                            nc.scalar.activation(hid[g % 2][:, j], hidden_banks(k, n), ACT.Gelu, bias=b1_s[:, e:e + 1]).then_inc(gelu_done, 1)

            pairs(act, pair)

        @block.vector
        def _(dve):
            for begun in (routeT_ready, fin_ready):
                dve.sem_inc(begun, START)

            def normalise(k, s):
                dve.wait_ge(rstd_step, 2 * s + 2)
                at_least(dve, ynT_done, s)
                for t in range(T2):
                    nc.vector.tensor_scalar(yn[:, t], y[k % 2][:, t], mv[k % 2][:, t, 0:1], rstd[k % 2][:, t:t + 1],
                                            ALU.subtract, ALU.mult).then_inc(yn_ready, 1)

            def logit_differences(s):
                dve.wait_ge(logits_done, s + 1)
                grouped = psum[:, B_LOGIT, 0:T2 * HE].rearrange("p (g e) -> p g e", e=EXPERTS)
                at_least(dve, ldiff_ready, s)
                nc.vector.tensor_reduce(lmax[:], grouped, AX_X, ALU.max).then_inc(lmax_ready, 1)
                dve.wait_ge(lmax_ready, s + 1)
                dst = ldiff[:, bass.ds(s, 1)].rearrange("p a (g e) -> p (a g) e", e=EXPERTS)
                nc.vector.tensor_tensor(dst, grouped, lmax[:].unsqueeze(2).to_broadcast([P, T2 * HEADS, EXPERTS]), ALU.subtract).then_inc(ldiff_ready, 1)

            def low_parts(b, k):
                s = RING * b + k
                dve.wait_ge(hT_ready, 2 * s + 2)
                dve.wait_ge(hi_ready, 2 * s + 2)
                from_start(dve, parts_stored[k % 2], 16 * 2 * CC * (2 * b + k // 2))
                nc.vector.tensor_tensor(lo[k % 2][:], hT[k % 2], hi[k % 2][:].bitcast(F32), ALU.subtract).then_inc(lo_ready, 1)

            def residual_and_statistics(k, s):
                dve.wait_ge(y_done, s + 1)
                dve.wait_ge(xb_ready, 2 * s + 2)
                nc.vector.tensor_tensor(y[k % 2][:].rearrange("p t d -> p (t d)"), psum[:, B_Y],
                                        xb[k % 2][:].rearrange("p t d -> p (t d)"), ALU.add).then_inc(y_ready, 1)
                dve.wait_ge(y_ready, s + 1)
                at_least(dve, mv_ready, 2 * s)
                for t in range(T2):
                    nc.vector.bn_stats(stats[:, t], y[k % 2][:, t]).then_inc(stats_ready, 1)
                dve.wait_ge(stats_ready, 2 * s + 2)
                carried(dve, dve_ticks)
                for t in range(T2):
                    nc.vector.bn_aggr(mv[k % 2][:, t], stats[:, t]).then_inc(mv_ready, 1)

            def by_head(t):
                return t[:].rearrange("p (g e) -> p g e", e=EXPERTS)

            def wide(t):
                return t[:].unsqueeze(2).to_broadcast([P, T2 * HEADS, EXPERTS])

            def choose_two(s, part):
                probs = prob[:, bass.ds(s, 1)].rearrange("p a n -> p (a n)")
                diff = ldiff[:, bass.ds(s, 1)].rearrange("p a n -> p (a n)")
                v = nc.vector
                done = [(0, 4, 8, 11)[part]]

                def own(ins):
                    done[0] += 1
                    ins.then_inc(choose_step, 1)
                    dve.wait_ge(choose_step, CHOOSE * s + done[0])

                if part == 0:
                    dve.wait_ge(prob_ready, s + 1)
                    own(v.scalar_tensor_tensor(out=t_s[:], in0=diff, scalar=0.0, in1=rank_s[:], op0=ALU.is_equal, op1=ALU.mult))
                    own(v.tensor_reduce(t_m[:], by_head(t_s), AX_X, ALU.max))
                    own(v.tensor_tensor(by_head(t_one), by_head(t_s), wide(t_m), ALU.is_equal))
                    own(v.scalar_tensor_tensor(out=t_rest[:], in0=t_one[:], scalar=-1e30, in1=diff, op0=ALU.mult, op1=ALU.add))
                elif part == 1:
                    own(v.tensor_reduce(t_m[:], by_head(t_rest), AX_X, ALU.max))
                    own(v.tensor_tensor(by_head(t_q), by_head(t_rest), wide(t_m), ALU.is_equal))
                    own(v.tensor_tensor(t_s[:], t_q[:], rank_s[:], ALU.mult))
                    own(v.tensor_reduce(t_m[:], by_head(t_s), AX_X, ALU.max))
                elif part == 2:
                    own(v.tensor_tensor(by_head(t_two), by_head(t_s), wide(t_m), ALU.is_equal))
                    carried(dve, dve_ticks)
                    own(v.tensor_reduce(t_z[:], prob[:, bass.ds(s, 1)].rearrange("p a (g e) -> p (a g) e", e=EXPERTS), AX_X, ALU.add))
                    own(v.reciprocal(t_rz[:], t_z[:]))
                else:
                    own(v.tensor_tensor(t_two[:], t_one[:], t_two[:], ALU.add))
                    own(v.tensor_tensor(t_q[:], t_two[:], probs, ALU.mult))
                    from_start(dve, routeT_done, s)
                    own(v.tensor_tensor(by_head(route), by_head(t_q), wide(t_rz), ALU.mult))

            def evacuate_routeT(s):
                from_start(dve, routeT_done, s + 1)
                from_start(dve, route_stored, 16 * s)
                nc.vector.tensor_copy(routeT[:], psum[:, B_AUX, 0:TOK]).then_inc(routeT_ready, 1)

            def step(b, k):
                s = RING * b + k
                one, three = back(b, k, 1), back(b, k, 3)
                if within(*one):
                    residual_and_statistics(one[1], s - 1)
                if within(*three):
                    low_parts(*three)
                    logit_differences(s - 3)
                if within(*one):
                    normalise(one[1], s - 1)
                if choosing(b):
                    for i, part in (((0, 0), (0, 1), (0, 2)), ((0, 3), (1, 0), (1, 1)), ((1, 2), (1, 3)), ())[k]:
                        choose_two(2 * b - 2 + i, part)
                    if k >= 2:
                        evacuate_routeT(2 * b + k - 4)

            def split_w1():
                dve.wait_ge(tail_consts, 16 * 11)
                nc.vector.tensor_copy(w1_s[:], w1_raw).then_inc(w1_high, 1)
                dve.wait_ge(w1_high, 1)
                nc.vector.tensor_tensor(w1_s[P // 2:P], w1_raw[P // 2:P], w1_s[P // 2:P].bitcast(F32), ALU.subtract).then_inc(w1_split, 1)

            steps(step, dve, between=split_w1)

            def weight(u, k, g, h):
                dve.wait_ge(expert_done, 2 * (GROUPS * u + g) + h + 1)
                if h == 0 and g == 0:
                    dve.wait_ge(wb_loaded, 16 * (u + 1))
                if h == 0:
                    at_least(dve, summed, 3 * (u - 1) + max(g, 1))
                cols = slice(h * HALF, (h + 1) * HALF)
                nc.vector.scalar_tensor_tensor(out=wout[:, g, cols], in0=psum[:, B_OUT], scalar=b2_s[:, g:g + 1],
                                               in1=wb[k][:, g, cols], op0=ALU.add, op1=ALU.mult).then_inc(weighted, 1)

            def evacuate_mixed(u, k):
                dve.wait_ge(mixed_done, u + 1)
                from_start(dve, mixed_stored, 16 * (u - 1))
                nc.vector.tensor_copy(mixed[k][:], psum[:, B_AUX, 0:TOK]).then_inc(mixed_ready, 1)

            def finish_rows(s, bank, rows, dst):
                from_start(dve, proj_done, s + 1)
                dve.wait_ge(xres_biased, 2 * s + 2)
                nc.vector.tensor_tensor(dst[:].rearrange("p t d -> p (t d)"), psum[:, bank],
                                        rows[:].rearrange("p t d -> p (t d)"), ALU.add).then_inc(fin_ready, 1)

            def pair(p, choose, project):
                for k in range(2):
                    u = 2 * p + k
                    first = isinstance(p, int) and u == 0
                    for g in range(GROUPS):
                        before = None if first and g == 0 else (u, k, g - 1) if g else (u - 1, 1 - k, GROUPS - 1)
                        if before:
                            weight(*before, 0)
                        if choose and k == 0:
                            choose_two(p + LEAD, g)
                        if before:
                            weight(*before, 1)
                        if (k, g) == (0, 2) and not first:
                            evacuate_mixed(u - 1, 1)
                        if choose and (k, g) == (1, 0):
                            evacuate_routeT(p + LEAD)
                        if project and (k, g) == (1, 1):
                            from_start(dve, out_stored, 16 * (p - LAG))
                            finish_rows(p - LAG, B_AUX, xres, fin)
                        if (k, g) == (1, 3):
                            evacuate_mixed(u - 1, 0)

            pairs(dve, pair)
            for h in range(2):
                weight(UNITS - 1, 1, GROUPS - 1, h)
            evacuate_mixed(UNITS - 1, 1)
            for i in range(SPC):
                finish_rows(SAMPLES - SPC + i, i, xres_last[i], fin_last[i])

        @block.tensor
        def _(pe):
            for begun in (routeT_done, proj_done):
                pe.sem_inc(begun, START)

            def router(k, s):
                pe.wait_ge(hT_ready, 2 * s + 2)
                at_least(pe, ldiff_ready, s)
                for t in range(T2):
                    for c in range(CC):
                        at = t * HE + c * HPT * EXPERTS
                        last = nc.tensor.matmul(psum[:, B_LOGIT, at:at + HPT * EXPERTS], hT[k % 2][:, c, t * P:(t + 1) * P],
                                                emb_s[:], start=True, stop=True)
                last.then_inc(logits_done, 1)

            def turn_x(b, k, s):
                pe.wait_ge(x_loaded[k], 16 * (b + 1))
                at_least(pe, xT_ready, s)
                for t in range(T2):
                    for c in range(CC):
                        at = c * TOK + t * P
                        last = nc.tensor.transpose(psum[:, B_XT, at:at + P], xin[k][:, t, c * P:(c + 1) * P], ident_s[:])
                last.then_inc(xT_done, 1)

            def turn_yn(s):
                pe.wait_ge(yn_ready, 2 * s + 2)
                at_least(pe, ynT_ready, 2 * s)
                for t in range(T2):
                    for c in range(CC):
                        at = c * TOK + t * P
                        last = nc.tensor.transpose(psum[:, B_YNT, at:at + P], yn[:, t, c * P:(c + 1) * P], ident_s[:])
                last.then_inc(ynT_done, 1)

            def down(b, k, s):
                pe.wait_ge(xT_ready, s + 1)
                pe.wait_ge(pf_loaded[k], 16 * (b + 1))
                at_least(pe, z_ready, s)
                for c in range(CC):
                    last = nc.tensor.matmul(psum[:, B_Z, 0:TOK], pf[k][:, DOWN + c * NECK:DOWN + (c + 1) * NECK], xT[:, c],
                                            start=(c == 0), stop=(c == CC - 1))
                last.then_inc(z_done, 1)

            def project_heads(s):
                pe.wait_ge(ynT_ready, 2 * s + 2)
                at_least(pe, hT_ready, 2 * s)
                for o in range(CC):
                    for c in range(CC):
                        last = nc.tensor.matmul(psum[:, B_HT, o * TOK:(o + 1) * TOK], wm_s[:, c, o * P:(o + 1) * P], ynT[:, c],
                                                start=(c == 0), stop=(c == CC - 1))
                last.then_inc(hT_done, 1)

            def up(k, s):
                pe.wait_ge(z_ready, s + 1)
                at_least(pe, y_ready, s)
                for t in range(T2):
                    last = nc.tensor.matmul(psum[:, B_Y, t * D:(t + 1) * D], zT[:, t * P:(t + 1) * P], pf[k][:, UP:UP + D],
                                            start=True, stop=True)
                last.then_inc(y_done, 1)

            def turn_route(s):
                pe.wait_ge(choose_step, CHOOSE * (s + 1))
                from_start(pe, routeT_ready, s)
                for t in range(T2):
                    last = nc.tensor.transpose(psum[:, B_AUX, t * P:(t + 1) * P], route[:, t * HE:(t + 1) * HE], ident_s[:])
                last.then_inc(routeT_done, 1)

            def step(b, k):
                s = RING * b + k
                two, three = back(b, k, 2), back(b, k, 3)
                if within(b, k):
                    turn_x(b, k, s)
                if within(*two):
                    turn_yn(s - 2)
                if within(*three):
                    router(three[1], s - 3)
                if within(b, k):
                    down(b, k, s)
                if within(*two):
                    project_heads(s - 2)
                if within(b, k):
                    up(k, s)
                if choosing(b) and k >= 2:
                    turn_route(2 * b + k - 4)

            pe.wait_ge(head_consts, 16 * 4)
            steps(step, pe)
            pe.wait_ge(w1_split, 1)
            pe.wait_ge(prob_ready, SAMPLES)
            pe.wait_ge(tail_consts, 16 * 11)

            def hidden(u, k, n):
                e = GROUPS * (n % GE) + n // GE
                at_least(pe, gelu_done, EXPERTS * u + (n - 1 if k == 0 and n < 2 else n - 2))
                for h in range(2):
                    last = nc.tensor.matmul(hidden_banks(k, n)[:, h * HALF:(h + 1) * HALF], w1_s[:, e], parts[k][:, h * HALF:(h + 1) * HALF],
                                            start=True, stop=True)
                last.then_inc(hidden_done, 1)

            def experts(u, g, h):
                if h == 0:
                    pe.wait_ge(gelu_done, EXPERTS * u + GE * (g + 1))
                at_least(pe, weighted, 2 * (GROUPS * u + g) + h)
                for j in range(GE):
                    last = nc.tensor.matmul(psum[HD * j:HD * (j + 1), B_OUT], w2_s[:, GROUPS * j + g], hid[g % 2][:, j, h * HALF:(h + 1) * HALF],
                                            start=True, stop=True)
                last.then_inc(expert_done, 1)

            def mix(u, k):
                pe.wait_ge(summed, 3 * u + 3)
                for q in range(HPT):
                    last = nc.tensor.matmul(psum[HD * q:HD * (q + 1), B_AUX, 0:TOK], sel_s[:], total[k][:, q * TOK:(q + 1) * TOK],
                                            start=True, stop=True)
                last.then_inc(mixed_done, 1)

            def project_out(bank, t, mixed_rows, first_column):
                for c in range(CC):
                    at = first_column + t * P
                    last = nc.tensor.matmul(psum[:, bank, t * D:(t + 1) * D], mixed_rows[:, c, at:at + P], wo_s[:, c],
                                            start=(c == 0), stop=(c == CC - 1))
                if t == T2 - 1:
                    last.then_inc(proj_done, 1)

            def pair(p, choose, project):
                for k in range(2):
                    u = 2 * p + k
                    first = isinstance(p, int) and u == 0
                    pe.wait_ge(parts_loaded, 16 * (u + 1))
                    for g in range(GROUPS):
                        before = None if first and g == 0 else (u, g - 1) if g else (u - 1, GROUPS - 1)
                        for j in range(GE):
                            hidden(u, k, GE * g + j)
                            if j % 2 == 1 and before:
                                experts(*before, j // 2)
                            if (k, g, j) == (0, 2, 2) and not first:
                                from_start(pe, routeT_ready, p + LEAD if choose else SAMPLES)
                                pe.wait_ge(mixed_ready, u - 1)
                                mix(u - 1, 1)
                            if choose and (k, g, j) == (1, 0, 2):
                                at_least(pe, mixed_ready, u - 1)
                                turn_route(p + LEAD)
                            if project and (k, g) == (1, 1) and j >= 2:
                                if j == 2:
                                    pe.wait_ge(mixT_loaded, 16 * (p - LAG + 1))
                                    pe.wait_ge(mixed_ready, u - 1)
                                    if choose:
                                        from_start(pe, routeT_ready, p + LEAD + 1)
                                project_out(B_AUX, j - 2, mixT, 0)
                            if (k, g, j) == (1, 3, 2):
                                if project:
                                    from_start(pe, fin_ready, p - LAG + 1)
                                if choose:
                                    from_start(pe, routeT_ready, p + LEAD + 1)
                                at_least(pe, mixed_ready, u - 1)
                                mix(u - 1, 0)

            pairs(pe, pair)
            for h in range(2):
                experts(UNITS - 1, GROUPS - 1, h)
            pe.wait_ge(mixed_ready, UNITS - 1)
            mix(UNITS - 1, 1)
            pe.wait_ge(gelu_done, EXPERTS * UNITS)
            pe.wait_ge(early_loaded, 32)
            for i in range(SPC):
                pe.wait_ge(last_loaded[i], 16)
                for t in range(T2):
                    project_out(i, t, mix_last, i * TOK)


def kernel(x, itok_B_0_6, L0_cond_down_w, L0_cond_down_b, L0_cond_up_w, L0_cond_up_b, L0_cond_ln_g, L0_cond_ln_b,
           L0_ffn_Wm, L0_ffn_bm, L0_ffn_expert_emb, L0_ffn_W1, L0_ffn_b1, L0_ffn_W2, L0_ffn_b2, L0_ffn_Wo, L0_ffn_bo):
    import numpy as np
    import concourse.bacc as bacc
    from concourse.bass_utils import run_bass_kernel_spmd

    def tiles(a):
        return np.asarray(a).reshape(-1, P, a.shape[-1]).transpose(1, 0, 2)

    def columns(a):
        return np.asarray(a).reshape(-1, P).T

    prof = np.zeros((PROFILES, P, PW), np.float32)
    for i in range(PROFILES):
        prof[i, :, DOWN:UP] = tiles(L0_cond_down_w[i]).reshape(P, -1)
        prof[i, :, UP:DB] = L0_cond_up_w[i]
        prof[i, :, DB] = L0_cond_down_b[i]
        prof[i, :, LG:LB] = columns(L0_cond_ln_g[i])
        prof[i, :, LB:UB] = columns(L0_cond_ln_b[i])
        prof[i, :, UB:] = L0_cond_up_b[i]
    emb = np.zeros((P, HPT * EXPERTS), np.float32)
    for h in range(HPT):
        emb[HD * h:HD * (h + 1), EXPERTS * h:EXPERTS * (h + 1)] = L0_ffn_expert_emb
    arrays = {
        "x": x, "ids": itok_B_0_6, "prof": prof, "wm": tiles(L0_ffn_Wm), "bm": columns(L0_ffn_bm), "emb": emb,
        "w1": L0_ffn_W1, "b1": np.asarray(L0_ffn_b1).T, "w2": np.asarray(L0_ffn_W2).transpose(1, 0, 2),
        "b2": np.asarray(L0_ffn_b2).reshape(GE, GROUPS, HD).transpose(0, 2, 1).reshape(P, GROUPS),
        "wo": tiles(L0_ffn_Wo), "bo": np.broadcast_to(np.asarray(L0_ffn_bo), (P, D)),
        "ident": np.eye(P, dtype=np.float32), "sel": np.tile(np.eye(HD, dtype=np.float32), (GE, 1)),
        "rank": np.tile(np.arange(EXPERTS, 0, -1, dtype=np.float32), (P, TOK // EXPERTS)),
    }
    nc = bacc.Bacc("TRN2", target_bir_lowering=False, num_devices=1)
    held, args = {}, []
    for name, a in arrays.items():
        a = np.ascontiguousarray(a)
        held[f"in_{name}"] = a
        args.append(nc.dram_tensor(f"in_{name}", a.shape, mybir.dt.from_np(a.dtype), kind="ExternalInput").ap())
    out = nc.dram_tensor("out_rows", (SAMPLES, TOK, D), F32, kind="ExternalOutput").ap()
    build(nc, *args, out)
    return run_bass_kernel_spmd(nc, [held], core_ids=[0]).results[0]["out_rows"]
```

```python
from contextlib import ExitStack

import concourse.bass as bass
from concourse import mybir

F32 = mybir.dt.float32
F32R = mybir.dt.float32r
I32 = mybir.dt.int32
ALU = mybir.AluOpType
ACT = mybir.ActivationFunctionType
AX_X = mybir.AxisListType.X

P = 128
SAMPLES, TOK, D = 16, 256, 256
T2 = TOK // P
CC = D // P
PROFILES, NECK = 8, 128
HEADS, HD = 8, 32
EXPERTS, HID = 16, 128
EPS = 1e-5
CHUNK = 1024
SPC = CHUNK // TOK
CHUNKS = SAMPLES // SPC
UNITS = CHUNKS * HEADS
HALF = 512
GROUPS, GE = 4, 4
HPT = P // HD
HE = HEADS * EXPERTS
RING = 4
LEAD = 4
LAG = SPC
TAIL = 3
START = 1
CHOOSE = 14
PROJECT_AT = (1, 0), (1, 2), (2, 0), (2, 2)

DOWN, UP, DB, LG, LB, UB = 0, 256, 512, 513, 515, 517
PW = UB + D


def at_least(eng, sem, value):
    if not isinstance(value, int) or value > 0:
        eng.wait_ge(sem, value)


def from_start(eng, sem, value):
    if not isinstance(value, int) or value > 0:
        eng.wait_ge(sem, value + START)


def carried(eng, ticks):
    eng.sem_inc(ticks, 1)


def build(nc, x, ids, prof, wm, bm, emb, w1, b1, w2, b2, wo, bo, ident, sel, rank, out):
    with ExitStack() as ctx:
        def sb(name, shape, dt=F32):
            return ctx.enter_context(nc.sbuf_tensor(name, shape, dt))

        def sem(name):
            return ctx.enter_context(nc.semaphore(name))

        parts_d = nc.dram_tensor("parts_scratch", (CHUNKS, HEADS, 2, HD, CHUNK), F32, kind="Internal").ap()
        route_d = nc.dram_tensor("route_scratch", (CHUNKS, HE, CHUNK), F32, kind="Internal").ap()
        mixed_d = nc.dram_tensor("mixed_scratch", (CHUNKS, HEADS * HD, CHUNK), F32, kind="Internal").ap()

        psum = ctx.enter_context(nc.psum_tensor("psum", [P, 8, HALF], F32))

        ids_s = sb("ids_s", [1, SAMPLES], I32)
        wm_s = sb("wm_s", [P, CC, D])
        bm_s = sb("bm_s", [P, CC])
        emb_s = sb("emb_s", [P, HPT * EXPERTS])
        w1_s = sb("w1_s", [P, EXPERTS, HID], F32R)
        b1_s = sb("b1_s", [P, EXPERTS])
        w2_s = sb("w2_s", [P, EXPERTS, HD])
        b2_s = sb("b2_s", [P, GROUPS])
        wo_s = sb("wo_s", [P, CC, D])
        bo_s = sb("bo_s", [P, D])
        ident_s = sb("ident_s", [P, P])
        sel_s = sb("sel_s", [P, HD])
        rank_s = sb("rank_s", [P, TOK])
        minus_half = sb("minus_half", [P, T2])
        eps_s = sb("eps_s", [P, T2])

        xin = [sb(f"xin{i}", [P, T2, D]) for i in range(RING)]
        pf = [sb(f"pf{i}", [P, PW]) for i in range(RING)]
        xb = [sb(f"xb{i}", [P, T2, D]) for i in range(2)]
        zT = sb("zT", [P, TOK])
        y = [sb(f"y{i}", [P, T2, D]) for i in range(2)]
        stats = sb("stats", [P, T2, 6])
        mv = [sb(f"mv{i}", [P, T2, 2]) for i in range(2)]
        vareps = sb("vareps", [P, T2])
        rstd = [sb(f"rstd{i}", [P, T2]) for i in range(2)]
        yn = sb("yn", [P, T2, D])
        mix_last = sb("mix_last", [P, CC, CHUNK])
        hT = [mix_last[:, i, 0:HALF].rearrange("p (c t) -> p c t", c=CC) for i in range(2)]
        xT, ynT = (mix_last[:, i, HALF:CHUNK].rearrange("p (c t) -> p c t", c=CC) for i in range(2))
        hi = [sb(f"hi{i}", [P, CC, TOK], F32R) for i in range(2)]
        lo = [sb(f"lo{i}", [P, CC, TOK], F32R) for i in range(2)]
        lmax = sb("lmax", [P, T2 * HEADS])
        ldiff = sb("ldiff", [P, SAMPLES, T2 * HE])
        prob = sb("prob", [P, SAMPLES, T2 * HE])

        t_q = sb("t_q", [P, T2 * HE])
        t_s = sb("t_s", [P, T2 * HE])
        t_one = sb("t_one", [P, T2 * HE])
        t_rest = sb("t_rest", [P, T2 * HE])
        t_two = sb("t_two", [P, T2 * HE])
        t_m = sb("t_m", [P, T2 * HEADS])
        t_z = sb("t_z", [P, T2 * HEADS])
        t_rz = sb("t_rz", [P, T2 * HEADS])
        route = sb("route", [P, T2 * HE])
        routeT = sb("routeT", [P, TOK])

        parts = [sb(f"parts{i}", [P, CHUNK], F32R) for i in range(2)]
        wb = [sb(f"wb{i}", [P, GROUPS, CHUNK]) for i in range(2)]
        hid = [sb(f"hid{i}", [P, GE, CHUNK]) for i in range(2)]
        w1_raw = hid[0][:, 0:2].rearrange("p a (e i) -> p (a e) i", i=HID)
        wout = sb("wout", [P, GROUPS, CHUNK])
        total = [sb(f"total{i}", [P, CHUNK]) for i in range(2)]
        mixed = [sb(f"mixed{i}", [P, TOK]) for i in range(2)]
        mixT = sb("mixT", [P, CC, TOK])
        xres = sb("xres", [P, T2, D])
        fin = sb("fin", [P, T2, D])
        xres_last, fin_last = xin, xb + y
        wo_last = yn[:, 0]

        ids_loaded, ident_loaded = sem("ids_loaded"), sem("ident_loaded")
        head_consts, tail_consts = sem("head_consts"), sem("tail_consts")
        x_loaded = [sem(f"x_loaded{i}") for i in range(RING)]
        pf_loaded = [sem(f"pf_loaded{i}") for i in range(RING)]
        parts_stored = [sem(f"parts_stored{i}") for i in range(2)]
        route_stored, mixed_stored, out_stored = sem("route_stored"), sem("mixed_stored"), sem("out_stored")
        parts_loaded, wb_loaded = sem("parts_loaded"), sem("wb_loaded")
        wb_first_loaded = [sem(f"wb_first_loaded{h}") for h in range(2)]
        mixT_loaded, xres_loaded = sem("mixT_loaded"), sem("xres_loaded")
        xres_last_loaded = sem("xres_last_loaded")
        wo_last_loaded = sem("wo_last_loaded")
        mix_low_loaded, mix_high_loaded = sem("mix_low_loaded"), sem("mix_high_loaded")
        half_set = sem("half_set")
        sp_ticks, dve_ticks = sem("sp_ticks"), sem("dve_ticks")
        w1_high, w1_split = sem("w1_high"), sem("w1_split")
        xb_ready = sem("xb_ready")
        xT_done, xT_ready = sem("xT_done"), sem("xT_ready")
        z_done, z_ready = sem("z_done"), sem("z_ready")
        y_done, y_ready = sem("y_done"), sem("y_ready")
        stats_ready, mv_ready = sem("stats_ready"), sem("mv_ready")
        rstd_step = sem("rstd_step")
        yn_ready = sem("yn_ready")
        ynT_done, ynT_ready = sem("ynT_done"), sem("ynT_ready")
        hT_done, hT_ready = sem("hT_done"), sem("hT_ready")
        hi_ready, lo_ready = sem("hi_ready"), sem("lo_ready")
        logits_done, lmax_ready, ldiff_ready = sem("logits_done"), sem("lmax_ready"), sem("ldiff_ready")
        prob_ready = sem("prob_ready")
        choose_step = sem("choose_step")
        routeT_done, routeT_ready = sem("routeT_done"), sem("routeT_ready")
        hidden_done = sem("hidden_done")
        gelu_done = sem("gelu_done")
        expert_done = sem("expert_done")
        weighted = sem("weighted")
        summed = sem("summed")
        mixed_done, mixed_ready = sem("mixed_done"), sem("mixed_ready")
        last_summed = sem("last_summed")
        proj_done, xres_biased, fin_ready = sem("proj_done"), sem("xres_biased"), sem("fin_ready")

        B_XT, B_Z, B_Y, B_YNT, B_HT, B_LOGIT = range(6)
        B_OUT, B_AUX = 6, 7
        LAST_OUT, LAST_PROJ = (B_OUT, 1), (4, 5, B_AUX, 0)

        def back(b, k, lag):
            return b + (k - lag) // RING, (k - lag) % RING

        def steps(step, eng, between=None):
            for k in range(RING):
                step(0, k)
            if between:
                between()
            with eng.Fori(1, SAMPLES // RING) as b:
                for k in range(RING):
                    step(b, k)
            for k in range(TAIL):
                step(SAMPLES // RING, k)

        def within(b, k):
            return not isinstance(b, int) or 0 <= RING * b + k < SAMPLES

        def choosing(b):
            return not isinstance(b, int) or b > 0

        def turning(b, k):
            return choosing(b) and k == (TAIL - 1 if isinstance(b, int) else RING - 1)

        def pairs(eng, pair):
            chosen = (SAMPLES - LEAD) // 2
            pair(0, True, (False, True), False)
            with eng.Fori(1, LAG) as p:
                pair(p, True, (True, True), False)
            with eng.Fori(LAG, chosen) as p:
                pair(p, True, (True, True), True)
            pair(chosen, False, (True, False), True)
            with eng.Fori(chosen + 1, SAMPLES - 1) as p:
                pair(p, False, (False, False), True)
            pair(SAMPLES - 1, False, (False, False), True)

        def is_pair(p, which):
            return isinstance(p, int) and p == which

        def hidden_banks(k, n):
            i = (k + n) % 3
            return psum[:, 2 * i:2 * i + 2].rearrange("p b t -> p (b t)")

        block = ctx.enter_context(nc.Block())

        @block.sync
        def _(sp):
            for begun in (route_stored, mixed_stored, out_stored, *parts_stored):
                sp.sem_inc(begun, START)
            sp.dma_start(ids_s[:], ids.rearrange("(a n) -> a n", a=1)).then_inc(ids_loaded, 16)

            def load_x(b, k):
                s = RING * b + k
                at_least(sp, xb_ready, 2 * (s - RING + 1))
                at_least(sp, xT_done, s - RING + 1)
                carried(sp, sp_ticks)
                sp.dma_start(xin[k][:], x[bass.ds(s, 1)].rearrange("a (t p) d -> p (a t) d", p=P)).then_inc(x_loaded[k], 16)

            def load_profile(b, k):
                s = RING * b + k
                at_least(sp, xb_ready, 2 * (s - RING + 1))
                at_least(sp, ynT_ready, 2 * (s - RING + 1))
                at_least(sp, y_done, s - RING + 1)
                carried(sp, sp_ticks)
                pid = sp.value_load(ids_s[0:1, bass.ds(s, 1)], min_val=0, max_val=PROFILES - 1)
                sp.dma_start(pf[k][:], prof[bass.ds(pid, 1)].rearrange("a p n -> (a p) n")).then_inc(pf_loaded[k], 16)

            def store_parts(b, k):
                s = RING * b + k
                for l, (ready, n, buf) in enumerate(((hi_ready, 2 * s + 2, hi), (lo_ready, s + 1, lo))):
                    sp.wait_ge(ready, n)
                    carried(sp, sp_ticks)
                    for c in range(CC):
                        dst = parts_d[bass.ds(b, 1), HPT * c:HPT * (c + 1), l, :, k * TOK:(k + 1) * TOK]
                        sp.dma_start(dst.rearrange("a h d t -> (a h) d t"),
                                     buf[k % 2][:, c, :].bitcast(F32)).then_inc(parts_stored[k % 2], 16)

            load_x(0, 0)
            sp.dma_start(ident_s[:], ident).then_inc(ident_loaded, 16)
            sp.wait_ge(ids_loaded, 16)
            load_profile(0, 0)
            load_x(0, 1)
            load_profile(0, 1)
            for dst, src in ((wm_s, wm), (bm_s, bm), (emb_s, emb)):
                sp.dma_start(dst[:], src).then_inc(head_consts, 16)
            def load_tail_consts():
                for q in range(P // HD):
                    sp.dma_start(w1_raw[HD * q:HD * (q + 1)], w1.rearrange("e d i -> d e i")).then_inc(tail_consts, 16)
                for dst, src in ((b1_s, b1), (w2_s, w2), (b2_s, b2), (wo_s, wo), (bo_s, bo), (sel_s, sel), (rank_s, rank)):
                    sp.dma_start(dst[:], src).then_inc(tail_consts, 16)

            def step(b, k):
                ahead = (b, k + 2) if k < 2 else (b + 1, k - 2)
                if within(*ahead):
                    load_x(*ahead)
                    load_profile(*ahead)
                if within(*back(b, k, 3)):
                    store_parts(*back(b, k, 3))
                if turning(b, k):
                    store_route(b - 1)

            def store_route(s):
                from_start(sp, routeT_ready, s + 1)
                carried(sp, sp_ticks)
                from_start(sp, route_stored, 16 * s)
                carried(sp, sp_ticks)
                dst = route_d[bass.ds(s // SPC, 1), :, bass.ds((s % SPC) * TOK, TOK)]
                sp.dma_start(dst.rearrange("a r t -> (a r) t"), routeT[:]).then_inc(route_stored, 16)

            def load_parts(u, k):
                at_least(sp, hidden_done, EXPERTS * (u - 1))
                at_least(sp, parts_loaded, 16 * u)
                carried(sp, sp_ticks)
                src = parts_d.rearrange("c h l d t -> (c h) (l d) t")[bass.ds(u, 1)]
                sp.dma_start(parts[k][:].bitcast(F32), src.to_broadcast([2, 2 * HD, CHUNK])).then_inc(parts_loaded, 16)

            def load_wb(u, k, stored):
                at_least(sp, weighted, 2 * GROUPS * (u - 1))
                at_least(sp, wb_loaded, 16 * (u - 1))
                from_start(sp, route_stored, 16 * stored)
                carried(sp, sp_ticks)
                src = route_d.rearrange("c (h j g) t -> (c h) j (g t)", h=HEADS, g=GROUPS)[bass.ds(u, 1)]
                src = src.rearrange("a j n -> j a n").to_broadcast([GE, HD, GROUPS * CHUNK])
                sp.dma_start(wb[k][:].rearrange("p g t -> p (g t)"), src).then_inc(wb_loaded, 16)

            def store_mixed(u, k):
                sp.wait_ge(mixed_ready, u + 1)
                carried(sp, sp_ticks)
                from_start(sp, mixed_stored, 16 * u)
                carried(sp, sp_ticks)
                dst = mixed_d.rearrange("c (h o) (q t) -> (c h) q o t", h=HEADS, q=HPT)[bass.ds(u, 1)]
                sp.dma_start(dst.rearrange("a q o t -> (a q) o t"), mixed[k][:]).then_inc(mixed_stored, 16)

            def load_back(s, stored):
                from_start(sp, mixed_stored, 16 * stored)
                carried(sp, sp_ticks)
                from_start(sp, proj_done, s)
                carried(sp, sp_ticks)
                src = mixed_d.rearrange("c (t r) n -> c r t n", r=P)[bass.ds(s // SPC, 1), :, :, bass.ds((s % SPC) * TOK, TOK)]
                sp.dma_start(mixT[:], src.rearrange("a r t n -> (a r) t n")).then_inc(mixT_loaded, 16)
                from_start(sp, fin_ready, s)
                carried(sp, sp_ticks)
                sp.dma_start(xres[:], x[bass.ds(s, 1)].rearrange("a (t p) d -> p (a t) d", p=P)).then_inc(xres_loaded, 16)

            def store_out(s):
                from_start(sp, fin_ready, s + 1)
                carried(sp, sp_ticks)
                sp.dma_start(out[bass.ds(s, 1)].rearrange("a (t p) d -> p (a t) d", p=P), fin[:]).then_inc(out_stored, 16)

            def last_block(b):
                for k in range(RING):
                    if k < 2:
                        load_x(b, k + 2)
                        load_profile(b, k + 2)
                    store_parts(*back(b, k, 3))
                store_route(b - 1)

            for k in range(RING):
                step(0, k)
                if k == 0:
                    load_tail_consts()
            with sp.Fori(1, SAMPLES // RING - 1) as b:
                for k in range(RING):
                    step(b, k)
            last_block(SAMPLES // RING - 1)
            def load_wb_half(h, stored):
                from_start(sp, route_stored, 16 * stored)
                cols = slice(h * HALF, (h + 1) * HALF)
                src = route_d[0, 0:EXPERTS, cols].rearrange("(j a g) t -> j a g t", a=1, g=GROUPS)
                for j in range(GE):
                    sp.dma_start(wb[0][HD * j:HD * (j + 1), :, cols], src[j].to_broadcast([HD, GROUPS, HALF])).then_inc(wb_first_loaded[h], 16)

            step(SAMPLES // RING, 0)
            load_parts(0, 0)
            step(SAMPLES // RING, 1)
            load_wb_half(0, SPC // 2)
            step(SAMPLES // RING, 2)
            load_wb_half(1, SPC)
            load_parts(1, 1)
            for i in range(2):
                from_start(sp, parts_stored[i], 16 * 2 * CC * SAMPLES // 2)

            mixed_last = mixed_d[CHUNKS - 1].rearrange("(t r) n -> t r n", r=P)

            def last_rows():
                for i in range(SPC):
                    sp.dma_start(xres_last[i][:], x[SAMPLES - SPC + i].rearrange("(t p) d -> p t d", p=P)).then_inc(xres_last_loaded, 16)
                from_start(sp, mixed_stored, 16 * (UNITS - HPT))
                sp.dma_start(mix_last[:, 0], mixed_last[0]).then_inc(mix_low_loaded, 16)
                rows = wo[P - HD:P, CC - 1].rearrange("(a d) n -> a d n", a=1)
                sp.dma_start(wo_last, rows.to_broadcast([GE, HD, D])).then_inc(wo_last_loaded, 16)

            def pair(p, choose, turn, project):
                last = is_pair(p, SAMPLES - 1)
                if last:
                    last_rows()
                first = is_pair(p, 0)
                stored = LEAD if first else 2 * p + LEAD - 1 if turn[0] else SAMPLES
                if not first:
                    store_mixed(2 * p - 2, 0)
                    load_parts(2 * p + 1, 1)
                if turn[0]:
                    store_route(2 * p + LEAD - 1)
                load_wb(2 * p + 1, 1, stored)
                if not first:
                    store_mixed(2 * p - 1, 1)
                if project:
                    load_back(p - LAG, 2 * p)
                if turn[1]:
                    store_route(2 * p + LEAD)
                if not last:
                    load_parts(2 * p + 2, 0)
                    load_wb(2 * p + 2, 0, stored)
                if project:
                    store_out(p - LAG)

            pairs(sp, pair)
            store_mixed(UNITS - 2, 0)
            from_start(sp, mixed_stored, 16 * (UNITS - 1))
            sp.dma_start(mix_last[0:P - HD, 1], mixed_last[1, 0:P - HD]).then_inc(mix_high_loaded, 16)
            for i in range(SPC):
                from_start(sp, fin_ready, SAMPLES - SPC + i + 1)
                sp.dma_start(out[SAMPLES - SPC + i].rearrange("(t p) d -> p t d", p=P), fin_last[i][:]).then_inc(out_stored, 16)
            from_start(sp, out_stored, 16 * SAMPLES)

        @block.gpsimd
        def _(pool):
            nc.gpsimd.memset(minus_half[:], -0.5).then_inc(half_set, 1)
            nc.gpsimd.memset(eps_s[:], EPS).then_inc(half_set, 1)
            pool.wait_ge(half_set, 2)

            def add_up_bias(b, k):
                s = RING * b + k
                pool.wait_ge(x_loaded[k], 16 * (b + 1))
                pool.wait_ge(pf_loaded[k], 16 * (b + 1))
                at_least(pool, y_ready, s - 1)
                for t in range(T2):
                    nc.gpsimd.tensor_tensor(xb[k % 2][:, t], xin[k][:, t], pf[k][:, UB:UB + D], ALU.add).then_inc(xb_ready, 1)

            def inverse_deviation(b, k):
                s = RING * b + k
                pool.wait_ge(mv_ready, 2 * s + 2)
                at_least(pool, rstd_step, 2 * s)
                nc.gpsimd.tensor_tensor(vareps[:], mv[k % 2][:, :, 1], eps_s[:], ALU.add).then_inc(rstd_step, 1)
                pool.wait_ge(rstd_step, 2 * s + 1)
                at_least(pool, yn_ready, 2 * (s - 1))
                nc.gpsimd.tensor_tensor(rstd[k % 2][:], vareps[:], minus_half[:], ALU.pow).then_inc(rstd_step, 1)

            def low_parts(b, k):
                s = RING * b + k
                pool.wait_ge(hT_ready, 2 * s + 2)
                pool.wait_ge(hi_ready, 2 * s + 2)
                from_start(pool, parts_stored[k % 2], 16 * 2 * CC * (2 * b + k // 2))
                nc.gpsimd.tensor_tensor(lo[k % 2][:], hT[k % 2], hi[k % 2][:].bitcast(F32), ALU.subtract).then_inc(lo_ready, 1)

            def step(b, k):
                if within(b, k):
                    add_up_bias(b, k)
                if within(*back(b, k, 1)):
                    inverse_deviation(*back(b, k, 1))
                if within(*back(b, k, 3)):
                    low_parts(*back(b, k, 3))

            steps(step, pool)

            def sum_groups(u, k, groups=GROUPS):
                pool.wait_ge(weighted, 2 * GROUPS * u + 4)
                at_least(pool, mixed_done, u - 1)
                nc.gpsimd.tensor_tensor(total[k][:], wout[:, 0], wout[:, 1], ALU.add).then_inc(summed, 1)
                for g in range(2, groups):
                    pool.wait_ge(weighted, 2 * GROUPS * u + 2 * g + 2)
                    pool.wait_ge(summed, 3 * u + g - 1)
                    nc.gpsimd.tensor_tensor(total[k][:], total[k][:], wout[:, g], ALU.add).then_inc(summed, 1)

            def bias_residual(s, rows):
                for t in range(T2):
                    nc.gpsimd.tensor_tensor(rows[:, t], rows[:, t], bo_s[:], ALU.add).then_inc(xres_biased, 1)

            def pair(p, choose, turn, project):
                sum_groups(2 * p, 0)
                if project:
                    pool.wait_ge(xres_loaded, 16 * (p - LAG + 1))
                    bias_residual(p - LAG, xres)
                sum_groups(2 * p + 1, 1, GROUPS - 1 if is_pair(p, SAMPLES - 1) else GROUPS)

            pool.wait_ge(tail_consts, 16 * 11)
            pairs(pool, pair)
            pool.wait_ge(xres_last_loaded, 16 * SPC)
            for i in range(SPC):
                bias_residual(SAMPLES - SPC + i, xres_last[i])

        @block.scalar
        def _(act):
            def evacuate_xT(s):
                act.wait_ge(xT_done, s + 1)
                at_least(act, z_done, s)
                nc.scalar.activation(xT.rearrange("p c t -> p (c t)"), psum[:, B_XT], ACT.Identity).then_inc(xT_ready, 1)

            def evacuate_z(k, s):
                act.wait_ge(z_done, s + 1)
                at_least(act, y_done, s)
                nc.scalar.activation(zT[:], psum[:, B_Z, 0:TOK], ACT.Relu, bias=pf[k][:, DB:DB + 1]).then_inc(z_ready, 1)

            def scale_ynT(k, s):
                act.wait_ge(ynT_done, s + 1)
                at_least(act, hT_done, s)
                for c in range(CC):
                    nc.scalar.activation(ynT[:, c], psum[:, B_YNT, c * TOK:(c + 1) * TOK], ACT.Identity,
                                         bias=pf[k][:, LB + c:LB + c + 1], scale=pf[k][:, LG + c:LG + c + 1]).then_inc(ynT_ready, 1)

            def evacuate_hT(b, k):
                s = RING * b + k
                if isinstance(s, int) and s == 0:
                    act.wait_ge(head_consts, 16 * 3)
                act.wait_ge(hT_done, s + 1)
                at_least(act, logits_done, s - 1)
                at_least(act, lo_ready, s - 1)
                from_start(act, parts_stored[k % 2], 16 * 2 * CC * (2 * b + k // 2))
                for c in range(CC):
                    nc.scalar.activation(hT[k % 2][:, c], psum[:, B_HT, c * TOK:(c + 1) * TOK], ACT.Identity,
                                         bias=bm_s[:, c:c + 1]).then_inc(hT_ready, 1)
                    nc.scalar.activation(hi[k % 2][:, c], psum[:, B_HT, c * TOK:(c + 1) * TOK], ACT.Identity,
                                         bias=bm_s[:, c:c + 1]).then_inc(hi_ready, 1)

            def exponentials(s):
                act.wait_ge(ldiff_ready, s + 1)
                dst = prob[:, bass.ds(s, 1)].rearrange("p a n -> p (a n)")
                src = ldiff[:, bass.ds(s, 1)].rearrange("p a n -> p (a n)")
                nc.scalar.activation(dst, src, ACT.Exp).then_inc(prob_ready, 1)

            def step(b, k):
                s = RING * b + k
                two, three = back(b, k, 2), back(b, k, 3)
                if within(b, k):
                    evacuate_xT(s)
                if within(*two):
                    scale_ynT(two[1], s - 2)
                if within(b, k):
                    evacuate_z(k, s)
                if within(*two):
                    evacuate_hT(*two)
                if within(*three):
                    exponentials(s - 3)

            steps(step, act)
            act.wait_ge(tail_consts, 16 * 11)

            def pair(p, choose, turn, project):
                for k in range(2):
                    u = 2 * p + k
                    for g in range(GROUPS):
                        for j in range(GE):
                            n, e = GE * g + j, GROUPS * j + g
                            act.wait_ge(hidden_done, EXPERTS * u + n + 1)
                            if j == 0:
                                at_least(act, expert_done, 2 * (GROUPS * u + g - 1))
                            nc.scalar.activation(hid[g % 2][:, j], hidden_banks(k, n), ACT.Gelu, bias=b1_s[:, e:e + 1]).then_inc(gelu_done, 1)

            pairs(act, pair)

        @block.vector
        def _(dve):
            for begun in (routeT_ready, fin_ready):
                dve.sem_inc(begun, START)

            def normalise(k, s):
                dve.wait_ge(rstd_step, 2 * s + 2)
                at_least(dve, ynT_done, s)
                for t in range(T2):
                    nc.vector.tensor_scalar(yn[:, t], y[k % 2][:, t], mv[k % 2][:, t, 0:1], rstd[k % 2][:, t:t + 1],
                                            ALU.subtract, ALU.mult).then_inc(yn_ready, 1)

            def logit_differences(s):
                dve.wait_ge(logits_done, s + 1)
                grouped = psum[:, B_LOGIT, 0:T2 * HE].rearrange("p (g e) -> p g e", e=EXPERTS)
                at_least(dve, ldiff_ready, s)
                nc.vector.tensor_reduce(lmax[:], grouped, AX_X, ALU.max).then_inc(lmax_ready, 1)
                dve.wait_ge(lmax_ready, s + 1)
                dst = ldiff[:, bass.ds(s, 1)].rearrange("p a (g e) -> p (a g) e", e=EXPERTS)
                nc.vector.tensor_tensor(dst, grouped, lmax[:].unsqueeze(2).to_broadcast([P, T2 * HEADS, EXPERTS]), ALU.subtract).then_inc(ldiff_ready, 1)

            def residual_and_statistics(k, s):
                dve.wait_ge(y_done, s + 1)
                dve.wait_ge(xb_ready, 2 * s + 2)
                nc.vector.tensor_tensor(y[k % 2][:].rearrange("p t d -> p (t d)"), psum[:, B_Y],
                                        xb[k % 2][:].rearrange("p t d -> p (t d)"), ALU.add).then_inc(y_ready, 1)
                dve.wait_ge(y_ready, s + 1)
                at_least(dve, mv_ready, 2 * s)
                for t in range(T2):
                    nc.vector.bn_stats(stats[:, t], y[k % 2][:, t]).then_inc(stats_ready, 1)
                dve.wait_ge(stats_ready, 2 * s + 2)
                carried(dve, dve_ticks)
                for t in range(T2):
                    nc.vector.bn_aggr(mv[k % 2][:, t], stats[:, t]).then_inc(mv_ready, 1)

            def by_head(t):
                return t[:].rearrange("p (g e) -> p g e", e=EXPERTS)

            def wide(t):
                return t[:].unsqueeze(2).to_broadcast([P, T2 * HEADS, EXPERTS])

            def choose_two(s, n):
                probs = prob[:, bass.ds(s, 1)].rearrange("p a n -> p (a n)")
                diff = ldiff[:, bass.ds(s, 1)].rearrange("p a n -> p (a n)")
                v = nc.vector
                if n == 0:
                    dve.wait_ge(prob_ready, s + 1)
                if n == CHOOSE - 1:
                    from_start(dve, routeT_done, s)
                if n > 0:
                    dve.wait_ge(choose_step, CHOOSE * s + n)
                if n == 0:
                    last = v.scalar_tensor_tensor(out=t_s[:], in0=diff, scalar=0.0, in1=rank_s[:], op0=ALU.is_equal, op1=ALU.mult)
                if n == 1:
                    last = v.tensor_reduce(t_m[:], by_head(t_s), AX_X, ALU.max)
                if n == 2:
                    last = v.tensor_tensor(by_head(t_one), by_head(t_s), wide(t_m), ALU.is_equal)
                if n == 3:
                    last = v.scalar_tensor_tensor(out=t_rest[:], in0=t_one[:], scalar=-1e30, in1=diff, op0=ALU.mult, op1=ALU.add)
                if n == 4:
                    last = v.tensor_reduce(t_m[:], by_head(t_rest), AX_X, ALU.max)
                if n == 5:
                    last = v.tensor_tensor(by_head(t_q), by_head(t_rest), wide(t_m), ALU.is_equal)
                if n == 6:
                    last = v.tensor_tensor(t_s[:], t_q[:], rank_s[:], ALU.mult)
                if n == 7:
                    last = v.tensor_reduce(t_m[:], by_head(t_s), AX_X, ALU.max)
                if n == 8:
                    last = v.tensor_tensor(by_head(t_two), by_head(t_s), wide(t_m), ALU.is_equal)
                if n == 9:
                    carried(dve, dve_ticks)
                    last = v.tensor_reduce(t_z[:], prob[:, bass.ds(s, 1)].rearrange("p a (g e) -> p (a g) e", e=EXPERTS), AX_X, ALU.add)
                if n == 10:
                    last = v.reciprocal(t_rz[:], t_z[:])
                if n == 11:
                    last = v.tensor_tensor(t_two[:], t_one[:], t_two[:], ALU.add)
                if n == 12:
                    last = v.tensor_tensor(t_q[:], t_two[:], probs, ALU.mult)
                if n == 13:
                    last = v.tensor_tensor(by_head(route), by_head(t_q), wide(t_rz), ALU.mult)
                last.then_inc(choose_step, 1)

            def evacuate_routeT(s):
                from_start(dve, routeT_done, s + 1)
                from_start(dve, route_stored, 16 * s)
                nc.vector.tensor_copy(routeT[:], psum[:, B_AUX, 0:TOK]).then_inc(routeT_ready, 1)

            def step(b, k):
                s = RING * b + k
                one, three = back(b, k, 1), back(b, k, 3)
                if within(*one):
                    residual_and_statistics(one[1], s - 1)
                if within(*three):
                    logit_differences(s - 3)
                if within(*one):
                    normalise(one[1], s - 1)
                if choosing(b):
                    ends = (0, 7, 14, 14) if isinstance(b, int) else (0, 5, 10, 14, 14)
                    for n in range(ends[k], ends[k + 1]):
                        choose_two(b - 1, n)
                    if turning(b, k):
                        evacuate_routeT(b - 1)

            def split_w1():
                dve.wait_ge(tail_consts, 16 * 11)
                nc.vector.tensor_copy(w1_s[:], w1_raw).then_inc(w1_high, 1)
                dve.wait_ge(w1_high, 1)
                nc.vector.tensor_tensor(w1_s[P // 2:P], w1_raw[P // 2:P], w1_s[P // 2:P].bitcast(F32), ALU.subtract).then_inc(w1_split, 1)

            steps(step, dve, between=split_w1)

            def weight(u, k, g, h, bank=B_OUT):
                dve.wait_ge(expert_done, 2 * (GROUPS * u + g) + h + 1)
                if isinstance(u, int) and u == 0:
                    if g == 0:
                        dve.wait_ge(wb_first_loaded[h], 16 * GE)
                elif h == 0 and g == 0:
                    dve.wait_ge(wb_loaded, 16 * u)
                if h == 0:
                    at_least(dve, summed, 3 * (u - 1) + max(g, 1))
                cols = slice(h * HALF, (h + 1) * HALF)
                nc.vector.scalar_tensor_tensor(out=wout[:, g, cols], in0=psum[:, bank], scalar=b2_s[:, g:g + 1],
                                               in1=wb[k][:, g, cols], op0=ALU.add, op1=ALU.mult).then_inc(weighted, 1)

            def evacuate_mixed(u, k):
                dve.wait_ge(mixed_done, u + 1)
                from_start(dve, mixed_stored, 16 * (u - 1))
                nc.vector.tensor_copy(mixed[k][:], psum[:, B_AUX, 0:TOK]).then_inc(mixed_ready, 1)

            def finish_rows(s, bank, rows, dst):
                from_start(dve, proj_done, s + 1)
                dve.wait_ge(xres_biased, 2 * s + 2)
                nc.vector.tensor_tensor(dst[:].rearrange("p t d -> p (t d)"), psum[:, bank],
                                        rows[:].rearrange("p t d -> p (t d)"), ALU.add).then_inc(fin_ready, 1)

            def pair(p, choose, turn, project):
                for k in range(2):
                    u = 2 * p + k
                    first = isinstance(p, int) and u == 0
                    for g in range(GROUPS):
                        before = None if first and g == 0 else (u, k, g - 1) if g else (u - 1, 1 - k, GROUPS - 1)
                        if (k, g) == (1, 3):
                            if project:
                                from_start(dve, out_stored, 16 * (p - LAG))
                                finish_rows(p - LAG, B_AUX, xres, fin)
                            if is_pair(p, SAMPLES - 1):
                                evacuate_mixed(u - 1, 0)
                        for h in range(2):
                            if before:
                                weight(*before, h)
                            for n in range(2 * (2 * g + h), 2 * (2 * g + h) + 2):
                                if choose and n < CHOOSE:
                                    choose_two(u + LEAD, n)
                            if turn[k] and (g, h) == (0, 0):
                                evacuate_routeT(u + LEAD - 1)
                        if (k, g) == (0, 2) and not first:
                            evacuate_mixed(u - 1, 1)
                        if (k, g) == (1, 3) and not is_pair(p, SAMPLES - 1):
                            evacuate_mixed(u - 1, 0)

            pairs(dve, pair)
            for h in range(2):
                weight(UNITS - 1, 1, GROUPS - 1, h, LAST_OUT[h])
            dve.wait_ge(summed, 3 * UNITS - 1)
            dve.wait_ge(weighted, 2 * GROUPS * UNITS)
            for h in range(2):
                cols = slice(h * HALF, (h + 1) * HALF)
                nc.vector.tensor_tensor(total[1][:, cols], total[1][:, cols], wout[:, GROUPS - 1, cols], ALU.add).then_inc(last_summed, 1)
            for i in range(SPC):
                finish_rows(SAMPLES - SPC + i, LAST_PROJ[i], xres_last[i], fin_last[i])

        @block.tensor
        def _(pe):
            for begun in (routeT_done, proj_done):
                pe.sem_inc(begun, START)

            def router(k, s):
                pe.wait_ge(hT_ready, 2 * s + 2)
                at_least(pe, ldiff_ready, s)
                for t in range(T2):
                    for c in range(CC):
                        at = t * HE + c * HPT * EXPERTS
                        last = nc.tensor.matmul(psum[:, B_LOGIT, at:at + HPT * EXPERTS], hT[k % 2][:, c, t * P:(t + 1) * P],
                                                emb_s[:], start=True, stop=True)
                last.then_inc(logits_done, 1)

            def turn_x(b, k, s):
                pe.wait_ge(x_loaded[k], 16 * (b + 1))
                at_least(pe, xT_ready, s)
                for t in range(T2):
                    for c in range(CC):
                        at = c * TOK + t * P
                        last = nc.tensor.transpose(psum[:, B_XT, at:at + P], xin[k][:, t, c * P:(c + 1) * P], ident_s[:])
                last.then_inc(xT_done, 1)

            def turn_yn(s):
                pe.wait_ge(yn_ready, 2 * s + 2)
                at_least(pe, ynT_ready, 2 * s)
                for t in range(T2):
                    for c in range(CC):
                        at = c * TOK + t * P
                        last = nc.tensor.transpose(psum[:, B_YNT, at:at + P], yn[:, t, c * P:(c + 1) * P], ident_s[:])
                last.then_inc(ynT_done, 1)

            def down(b, k, s):
                pe.wait_ge(xT_ready, s + 1)
                pe.wait_ge(pf_loaded[k], 16 * (b + 1))
                at_least(pe, z_ready, s)
                for c in range(CC):
                    last = nc.tensor.matmul(psum[:, B_Z, 0:TOK], pf[k][:, DOWN + c * NECK:DOWN + (c + 1) * NECK], xT[:, c],
                                            start=(c == 0), stop=(c == CC - 1))
                last.then_inc(z_done, 1)

            def project_heads(s):
                if isinstance(s, int) and s == 0:
                    pe.wait_ge(head_consts, 16 * 3)
                pe.wait_ge(ynT_ready, 2 * s + 2)
                at_least(pe, hT_ready, 2 * s)
                for o in range(CC):
                    for c in range(CC):
                        last = nc.tensor.matmul(psum[:, B_HT, o * TOK:(o + 1) * TOK], wm_s[:, c, o * P:(o + 1) * P], ynT[:, c],
                                                start=(c == 0), stop=(c == CC - 1))
                last.then_inc(hT_done, 1)

            def up(k, s):
                pe.wait_ge(z_ready, s + 1)
                at_least(pe, y_ready, s)
                for t in range(T2):
                    last = nc.tensor.matmul(psum[:, B_Y, t * D:(t + 1) * D], zT[:, t * P:(t + 1) * P], pf[k][:, UP:UP + D],
                                            start=True, stop=True)
                last.then_inc(y_done, 1)

            def turn_route(s):
                pe.wait_ge(choose_step, CHOOSE * (s + 1))
                from_start(pe, routeT_ready, s)
                for t in range(T2):
                    last = nc.tensor.transpose(psum[:, B_AUX, t * P:(t + 1) * P], route[:, t * HE:(t + 1) * HE], ident_s[:])
                last.then_inc(routeT_done, 1)

            def step(b, k):
                s = RING * b + k
                two, three = back(b, k, 2), back(b, k, 3)
                if within(b, k):
                    turn_x(b, k, s)
                if within(*two):
                    turn_yn(s - 2)
                if within(*three):
                    router(three[1], s - 3)
                if within(b, k):
                    down(b, k, s)
                if within(*two):
                    project_heads(s - 2)
                if within(b, k):
                    up(k, s)
                if turning(b, k):
                    turn_route(b - 1)

            pe.wait_ge(ident_loaded, 16)
            steps(step, pe)
            pe.wait_ge(w1_split, 1)
            pe.wait_ge(tail_consts, 16 * 11)

            def phase_1_has_read(pair_of_banks):
                for reader, count in (((xT_ready, SAMPLES), (z_ready, SAMPLES)), ((y_ready, SAMPLES), (ynT_ready, 2 * SAMPLES)),
                                      ((hT_ready, 2 * SAMPLES), (hi_ready, 2 * SAMPLES), (ldiff_ready, SAMPLES)))[pair_of_banks]:
                    pe.wait_ge(reader, count)

            def hidden(u, k, n):
                e = GROUPS * (n % GE) + n // GE
                if isinstance(u, int) and u == 0 and n < 3:
                    phase_1_has_read(n)
                else:
                    pe.wait_ge(gelu_done, EXPERTS * u + (n - 1 if k == 0 and n < 2 else n - 2))
                for h in range(2):
                    last = nc.tensor.matmul(hidden_banks(k, n)[:, h * HALF:(h + 1) * HALF], w1_s[:, e], parts[k][:, h * HALF:(h + 1) * HALF],
                                            start=True, stop=True)
                last.then_inc(hidden_done, 1)

            def experts(u, g, h, bank=B_OUT):
                if h == 0:
                    pe.wait_ge(gelu_done, EXPERTS * u + GE * (g + 1))
                if bank == B_OUT:
                    at_least(pe, weighted, 2 * (GROUPS * u + g) + h)
                for j in range(GE):
                    last = nc.tensor.matmul(psum[HD * j:HD * (j + 1), bank], w2_s[:, GROUPS * j + g], hid[g % 2][:, j, h * HALF:(h + 1) * HALF],
                                            start=True, stop=True)
                last.then_inc(expert_done, 1)

            def mix(u, k):
                pe.wait_ge(summed, 3 * u + 3)
                for q in range(HPT):
                    last = nc.tensor.matmul(psum[HD * q:HD * (q + 1), B_AUX, 0:TOK], sel_s[:], total[k][:, q * TOK:(q + 1) * TOK],
                                            start=True, stop=True)
                last.then_inc(mixed_done, 1)

            def project_out(bank, t, c, mixed_rows, first_column):
                at = first_column + t * P
                last = nc.tensor.matmul(psum[:, bank, t * D:(t + 1) * D], mixed_rows[:, c, at:at + P], wo_s[:, c],
                                        start=(c == 0), stop=(c == CC - 1))
                if (t, c) == (T2 - 1, CC - 1):
                    last.then_inc(proj_done, 1)

            def pair(p, choose, turn, project):
                for k in range(2):
                    u = 2 * p + k
                    first = isinstance(p, int) and u == 0
                    pe.wait_ge(parts_loaded, 16 * (u + 1))
                    for g in range(GROUPS):
                        before = None if first and g == 0 else (u, g - 1) if g else (u - 1, GROUPS - 1)
                        for j in range(GE):
                            hidden(u, k, GE * g + j)
                            if j % 2 == 1 and before:
                                experts(*before, j // 2)
                            if (k, g, j) == (0, 2, 2) and not first:
                                from_start(pe, routeT_ready, u + LEAD if turn[0] else SAMPLES)
                                pe.wait_ge(mixed_ready, u - 1)
                                mix(u - 1, 1)
                            if turn[k] and (g, j) == (0, 1):
                                at_least(pe, mixed_ready, u - 1)
                                turn_route(u + LEAD - 1)
                            if project and k == 1 and (g, j) in PROJECT_AT:
                                part = PROJECT_AT.index((g, j))
                                if part == 0:
                                    pe.wait_ge(mixT_loaded, 16 * (p - LAG + 1))
                                    from_start(pe, routeT_ready, u + LEAD if turn[1] else SAMPLES)
                                    pe.wait_ge(mixed_ready, u - 1)
                                project_out(B_AUX, part // CC, part % CC, mixT, 0)
                            if (k, g, j) == (1, 3, 0 if is_pair(p, SAMPLES - 1) else 2):
                                if project:
                                    from_start(pe, fin_ready, p - LAG + 1)
                                else:
                                    from_start(pe, routeT_ready, u + LEAD)
                                at_least(pe, mixed_ready, u - 1)
                                mix(u - 1, 0)

            from_start(pe, routeT_ready, LEAD)
            pairs(pe, pair)

            def project_last(i, t, rows, weights, start=False, stop=False):
                at = i * TOK + t * P
                return nc.tensor.matmul(psum[:, LAST_PROJ[i], t * D:(t + 1) * D], rows[:, at:at + P], weights, start=start, stop=stop)

            def project_low(i, t):
                project_last(i, t, mix_last[:, 0], wo_s[:, 0], start=True)

            pe.wait_ge(mix_low_loaded, 16)
            pe.wait_ge(gelu_done, EXPERTS * UNITS - 2)
            project_low(0, 0)
            project_low(1, 0)
            experts(UNITS - 1, GROUPS - 1, 0)
            experts(UNITS - 1, GROUPS - 1, 1, LAST_OUT[1])
            pe.wait_ge(mixed_ready, UNITS - 1)
            project_low(2, 0)
            project_low(3, 0)
            pe.wait_ge(mix_high_loaded, 16)
            pe.wait_ge(wo_last_loaded, 16)
            for i in range(SPC):
                for t in range(T2):
                    if t > 0:
                        project_low(i, t)
                    project_last(i, t, mix_last[0:P - HD, 1], wo_s[0:P - HD, 1])
                    pe.wait_ge(last_summed, i // 2 + 1)
                    last = project_last(i, t, total[1], wo_last, stop=True)
                last.then_inc(proj_done, 1)


def kernel(x, itok_B_0_6, L0_cond_down_w, L0_cond_down_b, L0_cond_up_w, L0_cond_up_b, L0_cond_ln_g, L0_cond_ln_b,
           L0_ffn_Wm, L0_ffn_bm, L0_ffn_expert_emb, L0_ffn_W1, L0_ffn_b1, L0_ffn_W2, L0_ffn_b2, L0_ffn_Wo, L0_ffn_bo):
    import numpy as np
    import concourse.bacc as bacc
    from concourse.bass_utils import run_bass_kernel_spmd

    def tiles(a):
        return np.asarray(a).reshape(-1, P, a.shape[-1]).transpose(1, 0, 2)

    def columns(a):
        return np.asarray(a).reshape(-1, P).T

    prof = np.zeros((PROFILES, P, PW), np.float32)
    for i in range(PROFILES):
        prof[i, :, DOWN:UP] = tiles(L0_cond_down_w[i]).reshape(P, -1)
        prof[i, :, UP:DB] = L0_cond_up_w[i]
        prof[i, :, DB] = L0_cond_down_b[i]
        prof[i, :, LG:LB] = columns(L0_cond_ln_g[i])
        prof[i, :, LB:UB] = columns(L0_cond_ln_b[i])
        prof[i, :, UB:] = L0_cond_up_b[i]
    emb = np.zeros((P, HPT * EXPERTS), np.float32)
    for h in range(HPT):
        emb[HD * h:HD * (h + 1), EXPERTS * h:EXPERTS * (h + 1)] = L0_ffn_expert_emb
    arrays = {
        "x": x, "ids": itok_B_0_6, "prof": prof, "wm": tiles(L0_ffn_Wm), "bm": columns(L0_ffn_bm), "emb": emb,
        "w1": L0_ffn_W1, "b1": np.asarray(L0_ffn_b1).T, "w2": np.asarray(L0_ffn_W2).transpose(1, 0, 2),
        "b2": np.asarray(L0_ffn_b2).reshape(GE, GROUPS, HD).transpose(0, 2, 1).reshape(P, GROUPS),
        "wo": tiles(L0_ffn_Wo), "bo": np.broadcast_to(np.asarray(L0_ffn_bo), (P, D)),
        "ident": np.eye(P, dtype=np.float32), "sel": np.tile(np.eye(HD, dtype=np.float32), (GE, 1)),
        "rank": np.tile(np.arange(EXPERTS, 0, -1, dtype=np.float32), (P, TOK // EXPERTS)),
    }
    nc = bacc.Bacc("TRN2", target_bir_lowering=False, num_devices=1)
    held, args = {}, []
    for name, a in arrays.items():
        a = np.ascontiguousarray(a)
        held[f"in_{name}"] = a
        args.append(nc.dram_tensor(f"in_{name}", a.shape, mybir.dt.from_np(a.dtype), kind="ExternalInput").ap())
    out = nc.dram_tensor("out_rows", (SAMPLES, TOK, D), F32, kind="ExternalOutput").ap()
    build(nc, *args, out)
    return run_bass_kernel_spmd(nc, [held], core_ids=[0]).results[0]["out_rows"]
```
